# Optimizing a Trainium2 kernel written in Bass

```python
import numpy as np
import jax
import jax.numpy as jnp

def _softmax(x, axis=-1):
    return jax.nn.softmax(x, axis=axis)

def _gelu(x):
    return jax.nn.gelu(x, approximate=True)

def _silu(x):
    return jax.nn.silu(x)

def _sigmoid(x):
    return jax.nn.sigmoid(x)

def _layernorm(x, axis=-1, eps=1e-05):
    m = jnp.mean(x, axis=axis, keepdims=True)
    v = jnp.var(x, axis=axis, keepdims=True)
    return (x - m) / jnp.sqrt(v + eps)

def _scatter_add(tgt, idx, src, axis=0):
    return tgt.at[idx].add(src)

def _segment_sum(src, seg, n):
    return jax.ops.segment_sum(src, seg, n)
kernel_name = 'mk_xattn_ffn_d1_seqx_r4_fd9c96'

def setup_inputs(seed: int=0):
    np.random.seed(seed)
    _w = jnp.asarray

    def _rec_inputs():
        import jax
        import jax.numpy as jnp
        _rk = jax.random.key(seed)
        x = -0.0005207 + 1.001 * jax.random.normal(jax.random.fold_in(_rk, 1), (4, 512, 512), jnp.float32)
        _lenS = 512 - jax.random.randint(jax.random.fold_in(_rk, 7), (4,), 0, max(1, 512 // 4) + 1, jnp.int32)
        _lenS2 = 512 - jax.random.randint(jax.random.fold_in(_rk, 8), (4,), 0, max(1, 512 // 4) + 1, jnp.int32)
        _ctx_2048P = jax.random.normal(jax.random.fold_in(_rk, 12), (4, 16, 512), jnp.float32)
        _ctx_2048c = jax.random.dirichlet(jax.random.fold_in(_rk, 512), 0.3 * jnp.ones((16,), jnp.float32), (4, 512))
        _ctx_2048t = jnp.einsum('bsk,bkd->bsd', _ctx_2048c, _ctx_2048P)
        _ctx_2048t = _ctx_2048t * jax.lax.rsqrt(jnp.mean(jnp.square(_ctx_2048t)) + 1e-12) * 0.953939
        ctx_2048 = -5.72187e-05 + 0.999849 * (_ctx_2048t + 0.3 * jax.random.normal(jax.random.fold_in(_rk, 612), (4, 512, 512), jnp.float32))
        _validS = jnp.arange(512)[None, :] < _lenS[:, None]
        _validS2 = jnp.arange(512)[None, :] < _lenS2[:, None]
        _causal = jnp.tril(jnp.ones((512, 512), dtype=bool))
        mask_BxSx4224_bf0 = jnp.logical_not(jnp.ones((4, 512, 1056), dtype=bool))
        return (x, ctx_2048, mask_BxSx4224_bf0)
    x, ctx_2048, mask_BxSx4224_bf0 = _rec_inputs()

    def _L0_xattn_setup():
        import jax, jax.numpy as jnp
        import numpy as np
        import math
        DIM = 512
        B, Q_LEN, KV_LEN = (8, 128, 1024)
        key = jax.random.key(seed)
        ks = jax.random.split(key, 8)
        x = jax.random.normal(ks[0], (B, Q_LEN, DIM), dtype=jnp.float32)
        mask = jnp.zeros((B, Q_LEN, KV_LEN + Q_LEN), dtype=bool)
        k_cache = jax.random.normal(ks[1], (B, KV_LEN, DIM), dtype=jnp.float32)
        v_cache = jax.random.normal(ks[2], (B, KV_LEN, DIM), dtype=jnp.float32)
        scale = 1.0 / math.sqrt(DIM)
        wq = jax.random.normal(ks[3], (DIM, DIM), dtype=jnp.float32) * scale
        wk = jax.random.normal(ks[4], (DIM, DIM), dtype=jnp.float32) * scale
        wv = jax.random.normal(ks[5], (DIM, DIM), dtype=jnp.float32) * scale
        wo = jax.random.normal(ks[6], (DIM, DIM), dtype=jnp.float32) * scale
        return {'x': x, 'mask': mask, 'k_cache': k_cache, 'v_cache': v_cache, 'wq': wq, 'wk': wk, 'wv': wv, 'wo': wo}
    _L0_xattn_all = _L0_xattn_setup()
    _L0_xattn_in = {k: v for k, v in _L0_xattn_all.items() if k in ('wq', 'wk', 'wv', 'wo')}
    del _L0_xattn_all

    def _L0_ffn_setup():
        import jax, jax.numpy as jnp
        import numpy as np
        E = 64
        K = 6
        CAP = 128
        SCALE = 1.0
        H = 512
        I = 192
        SI = I * 2
        B, S = (2, 256)

        def _moe(x, gate_w, gate_up_proj, down_proj, shared_gate_w, shared_up_w, shared_down_w):
            b, s, h = x.shape
            T = b * s
            xf = x.reshape(T, h)
            scores = jax.nn.softmax(xf @ gate_w.T, axis=-1)
            topk_w, topk_idx = jax.lax.top_k(scores, K)
            topk_w = topk_w * SCALE
            flat_e = topk_idx.reshape(-1)
            order = jnp.argsort(flat_e)
            sorted_e = flat_e[order]
            sorted_tok = (order // K).astype(jnp.int32)
            sorted_w = topk_w.reshape(-1)[order]
            counts = jnp.zeros((E,), jnp.int32).at[flat_e].add(1)
            offsets = jnp.cumsum(counts) - counts
            pos = jnp.arange(T * K, dtype=jnp.int32) - offsets[sorted_e]
            buf_tok = jnp.full((E, CAP), T, jnp.int32).at[sorted_e, pos].set(sorted_tok, mode='drop')
            buf_w = jnp.zeros((E, CAP), x.dtype).at[sorted_e, pos].set(sorted_w, mode='drop')
            xp = jnp.concatenate([xf, jnp.zeros((1, h), x.dtype)], axis=0)
            gx = xp[buf_tok]
            gu = jnp.einsum('ech,ehi->eci', gx, gate_up_proj)
            g, u = jnp.split(gu, 2, axis=-1)
            hid = jax.nn.silu(g) * u
            eo = jnp.einsum('eci,eih->ech', hid, down_proj) * buf_w[..., None]
            routed = jnp.zeros((T + 1, h), x.dtype).at[buf_tok.reshape(-1)].add(eo.reshape(-1, h))[:T]
            shared = jax.nn.silu(xf @ shared_gate_w.T) * (xf @ shared_up_w.T) @ shared_down_w.T
            return (routed + shared).reshape(b, s, h)
        key = jax.random.key(seed)
        ks = jax.random.split(key, 7)
        x = jax.random.normal(ks[0], (B, S, H), jnp.float32)
        gate_w = jax.random.normal(ks[1], (E, H), jnp.float32) * 0.02
        gate_up_proj = jax.random.normal(ks[2], (E, H, 2 * I), jnp.float32) * 0.02
        down_proj = jax.random.normal(ks[3], (E, I, H), jnp.float32) * 0.02
        shared_gate_w = jax.random.normal(ks[4], (SI, H), jnp.float32) * 0.02
        shared_up_w = jax.random.normal(ks[5], (SI, H), jnp.float32) * 0.02
        shared_down_w = jax.random.normal(ks[6], (H, SI), jnp.float32) * 0.02
        return dict(x=x, gate_w=gate_w, gate_up_proj=gate_up_proj, down_proj=down_proj, shared_gate_w=shared_gate_w, shared_up_w=shared_up_w, shared_down_w=shared_down_w)
    _L0_ffn_all = _L0_ffn_setup()
    _L0_ffn_in = {k: v for k, v in _L0_ffn_all.items() if k in ('gate_w', 'gate_up_proj', 'down_proj', 'shared_gate_w', 'shared_up_w', 'shared_down_w')}
    del _L0_ffn_all
    return {'x': x, 'ctx_2048': ctx_2048, 'mask_BxSx4224_bf0': mask_BxSx4224_bf0, 'L0_xattn_wq': _L0_xattn_in['wq'], 'L0_xattn_wk': _L0_xattn_in['wk'], 'L0_xattn_wv': _L0_xattn_in['wv'], 'L0_xattn_wo': _L0_xattn_in['wo'], 'L0_ffn_gate_w': _L0_ffn_in['gate_w'], 'L0_ffn_gate_up_proj': _L0_ffn_in['gate_up_proj'], 'L0_ffn_down_proj': _L0_ffn_in['down_proj'], 'L0_ffn_shared_gate_w': _L0_ffn_in['shared_gate_w'], 'L0_ffn_shared_up_w': _L0_ffn_in['shared_up_w'], 'L0_ffn_shared_down_w': _L0_ffn_in['shared_down_w']}

def reference(x, ctx_2048, mask_BxSx4224_bf0, L0_xattn_wq, L0_xattn_wk, L0_xattn_wv, L0_xattn_wo, L0_ffn_gate_w, L0_ffn_gate_up_proj, L0_ffn_down_proj, L0_ffn_shared_gate_w, L0_ffn_shared_up_w, L0_ffn_shared_down_w):
    import jax
    import jax.numpy as jnp

    def _L0_xattn_ref(x, mask, k_cache, v_cache, wq, wk, wv, wo):
        import jax, jax.numpy as jnp
        import numpy as np
        import math
        DIM = 512
        B, Q_LEN, KV_LEN = (8, 128, 1024)
        q = jnp.einsum('bsd,ed->bse', x, wq)
        k_new = jnp.einsum('bsd,ed->bse', x, wk)
        v_new = jnp.einsum('bsd,ed->bse', x, wv)
        k = jnp.concatenate([k_cache, k_new], axis=1)
        v = jnp.concatenate([v_cache, v_new], axis=1)
        scale = 1.0 / math.sqrt(q.shape[-1])
        scores = jnp.einsum('bqd,bkd->bqk', q, k) * scale
        attn = jax.nn.softmax(scores, axis=-1)
        out = jnp.einsum('bqk,bkd->bqd', attn, v)
        return jnp.einsum('bqd,ed->bqe', out, wo)

    def _L0_ffn_ref(x, gate_w, gate_up_proj, down_proj, shared_gate_w, shared_up_w, shared_down_w):
        import jax, jax.numpy as jnp
        import numpy as np
        E = 64
        K = 6
        CAP = 128
        SCALE = 1.0
        H = 512
        I = 192
        SI = I * 2
        B, S = (2, 256)

        def _moe(x, gate_w, gate_up_proj, down_proj, shared_gate_w, shared_up_w, shared_down_w):
            b, s, h = x.shape
            T = b * s
            xf = x.reshape(T, h)
            scores = jax.nn.softmax(xf @ gate_w.T, axis=-1)
            topk_w, topk_idx = jax.lax.top_k(scores, K)
            topk_w = topk_w * SCALE
            flat_e = topk_idx.reshape(-1)
            order = jnp.argsort(flat_e)
            sorted_e = flat_e[order]
            sorted_tok = (order // K).astype(jnp.int32)
            sorted_w = topk_w.reshape(-1)[order]
            counts = jnp.zeros((E,), jnp.int32).at[flat_e].add(1)
            offsets = jnp.cumsum(counts) - counts
            pos = jnp.arange(T * K, dtype=jnp.int32) - offsets[sorted_e]
            buf_tok = jnp.full((E, CAP), T, jnp.int32).at[sorted_e, pos].set(sorted_tok, mode='drop')
            buf_w = jnp.zeros((E, CAP), x.dtype).at[sorted_e, pos].set(sorted_w, mode='drop')
            xp = jnp.concatenate([xf, jnp.zeros((1, h), x.dtype)], axis=0)
            gx = xp[buf_tok]
            gu = jnp.einsum('ech,ehi->eci', gx, gate_up_proj)
            g, u = jnp.split(gu, 2, axis=-1)
            hid = jax.nn.silu(g) * u
            eo = jnp.einsum('eci,eih->ech', hid, down_proj) * buf_w[..., None]
            routed = jnp.zeros((T + 1, h), x.dtype).at[buf_tok.reshape(-1)].add(eo.reshape(-1, h))[:T]
            shared = jax.nn.silu(xf @ shared_gate_w.T) * (xf @ shared_up_w.T) @ shared_down_w.T
            return (routed + shared).reshape(b, s, h)
        return _moe(x, gate_w, gate_up_proj, down_proj, shared_gate_w, shared_up_w, shared_down_w)
    x = x + _L0_xattn_ref(_layernorm(x, axis=-1), mask_BxSx4224_bf0, ctx_2048, ctx_2048, L0_xattn_wq, L0_xattn_wk, L0_xattn_wv, L0_xattn_wo)
    x = x + _L0_ffn_ref(_layernorm(x, axis=-1), L0_ffn_gate_w, L0_ffn_gate_up_proj, L0_ffn_down_proj, L0_ffn_shared_gate_w, L0_ffn_shared_up_w, L0_ffn_shared_down_w)
    return x

_drawn_inputs = setup_inputs


def setup_inputs(seed=0):
    import zlib

    import numpy as np

    out = dict(_drawn_inputs(seed))
    spreads = {}
    factors = {'L0_ffn_gate_w': 8.0,
     'L0_ffn_gate_up_proj': 8.0,
     'L0_ffn_down_proj': 8.0,
     'L0_ffn_shared_gate_w': 8.0,
     'L0_ffn_shared_up_w': 8.0,
     'L0_ffn_shared_down_w': 8.0}
    for name, (base, spread) in spreads.items():
        noise = np.random.default_rng([zlib.crc32(name.encode()), seed]).standard_normal(out[name].shape)
        drawn = base * np.exp(spread * noise) if base else spread * noise
        out[name] = jnp.asarray(drawn.astype(out[name].dtype))
    for name, factor in factors.items():
        out[name] = (out[name] * factor).astype(out[name].dtype)
    return out
```

```python
from contextlib import ExitStack

import numpy as np

import concourse.bass as bass
from concourse import mybir

F32 = mybir.dt.float32
F32R = mybir.dt.float32r
BF16 = mybir.dt.bfloat16
I32 = mybir.dt.int32
U32 = mybir.dt.uint32
ALU = mybir.AluOpType
ACT = mybir.ActivationFunctionType
AX = mybir.AxisListType

P = 128
B, S, D = 4, 512, 512
T = B * S
C = D // P
NT = S // P
KV = 2 * S
E, K, CAP = 64, 6, 128
I = 192
SI = 2 * I
SC = SI // P
EPS = 1e-5
SCALE = float(D) ** -0.5
ROWS = T + CAP
OVER = float(1 << 20)

GROUPS = (
    [("xnT", i) for i in range(NT)] + [("q", m) for m in range(C)] + [("k", m) for m in range(C)]
    + [("v", 0), ("v", 1), ("pT", 0), ("pT", 1), ("v", 2), ("pT", 2), ("pT", 3), ("v", 3)]
    + [("pT", n) for n in range(4, 2 * NT)]
    + [("av", m) for m in range(C)] + [("wo", i) for i in range(NT)] + [("x2T", i) for i in range(NT)]
    + [("logits", 0)] + [("g", m) for m in range(SC)] + [("pos", 0)] + [("u", m) for m in range(SC)]
    + [("down", i) for i in range(NT)]
)
BANKS = 4
PER = len(GROUPS)
assert PER % BANKS == 0
AT = {name: n for n, name in enumerate(GROUPS)}
SPLIT = [g for g in GROUPS if g[0] in ("xnT", "q", "k", "v", "pT", "av", "x2T")]
SPLIT_AT = {name: n for n, name in enumerate(SPLIT)}
ITEMS = ["wq", "wk", "ctxT", "wv", "ctx", "wo", "gate", "sg", "su", "sd"]
ITEM_AT = {name: n for n, name in enumerate(ITEMS)}
WSLOT = {"wq": 0, "wk": 1, "wv": 0, "wo": 1, "gate": 0, "sg": 1, "su": 0, "sd": 1}
WIDTH = {"gate": C * E, "sg": C * SI, "su": C * SI, "sd": SC * D}
NI = len(ITEMS)


def wait_alone(eng, sem, value, passed):
    eng.wait_ge(sem, value)
    eng.sem_inc(passed, 1)


def attention_and_shared(nc, ctx, t, table, x2_rows):
    def sb(name, shape, dt=F32):
        return ctx.enter_context(nc.sbuf_tensor(name, shape, dt))

    def sem(name):
        return ctx.enter_context(nc.semaphore(name))

    def pair(name, shape):
        return sb(name + "_hi", shape, F32R), sb(name + "_lo", shape, F32R)

    stage = sb("stage", [P, 2, C * D])
    w_hi, w_lo = pair("w", [P, 2, C * D])
    xnT = pair("xnT", [P, C, S])
    ctxT = pair("ctxT", [P, C, S])
    cx = pair("cx", [P, C, D])
    qT = pair("qT", [P, C, S])
    kT = pair("kT", [P, C, S])
    v = pair("v", [P, NT, D])
    pT = pair("pT", [P, KV // P, S])
    x2T = tuple(h[:, 0:C, :] for h in pT)
    hT = tuple(h[:, C:C + SC, :] for h in pT)
    pbuf = sb("pbuf", [P, 2, KV])
    x2 = pbuf[:, :, :].rearrange("p a (b d) -> p (a b) d", d=D)
    hid = x2
    xn = sb("xn", [P, NT, D])
    res = sb("res", [P, NT, D])
    ident = sb("ident", [P, P])
    before = sb("before", [P, P], BF16)
    ones = sb("ones", [P, P], BF16)
    iota_e = sb("iota_e", [P, E])
    half = sb("half", [P, NT])
    stats = sb("stats", [P, NT, 6])
    mv = sb("mv", [P, NT, 2])
    veps = sb("veps", [P, NT])
    rstd = sb("rstd", [P, NT])
    stats2 = sb("stats2", [P, NT, 6])
    mv2 = sb("mv2", [P, NT, 2])
    veps2 = sb("veps2", [P, NT])
    rstd2 = sb("rstd2", [P, NT])
    mx = sb("mx", [P, NT])
    negmax = sb("negmax", [P, NT])
    rowsum = sb("rowsum", [P, NT])
    rinv = sb("rinv", [P, NT])
    logits = sb("logits", [P, NT, E])
    top8 = sb("top8", [P, NT, 8])
    arg8 = sb("arg8", [P, NT, 8], U32)
    argf = sb("argf", [P, NT, 8])
    negtop = sb("negtop", [P, NT])
    e8 = sb("e8", [P, NT, 8])
    elogits = sb("elogits", [P, E])
    esum = sb("esum", [P, NT])
    einv = sb("einv", [P, NT])
    hot = sb("hot", [P, K, E])
    chosen = sb("chosen", [P, E])
    chosen_b = sb("chosen_b", [P, NT, E], BF16)
    earlier = sb("earlier", [P, NT + 1, E], BF16)
    posk = sb("posk", [P, NT, K])
    over = sb("over", [P, NT, K])
    slotf = sb("slotf", [P, NT, K])
    slot = sb("slot", [P, NT, K], I32)
    tok = sb("tok", [P, NT])
    rows = sb("rows", [P, NT, K, 2])

    bank = ctx.enter_context(nc.psum_tensor("bank", [P, BANKS, 512], F32))
    scores = ctx.enter_context(nc.psum_tensor("scores", [P, 2, KV], F32))

    stage_loaded = [sem("stage_loaded0"), sem("stage_loaded1")]
    item_high = sem("item_high")
    item_low = sem("item_low")
    x_loaded = sem("x_loaded")
    res_loaded = sem("res_loaded")
    group_full = sem("group_full")
    group_taken = sem("group_taken")
    high_done = sem("high_done")
    vec_step = sem("vec_step")
    xn_ready = sem("xn_ready")
    scores_full = sem("scores_full")
    negmax_ready = sem("negmax_ready")
    exp_done = sem("exp_done")
    var_ready = sem("var_ready")
    rstd_ready = sem("rstd_ready")
    x2_ready = sem("x2_ready")
    x2_stored = sem("x2_stored")
    negtop_ready = sem("negtop_ready")
    router_exp = sem("router_exp")
    chosen_ready = sem("chosen_ready")
    silu_done = sem("silu_done")
    hid_ready = sem("hid_ready")
    hid_high = sem("hid_high")
    hT_ready = sem("hT_ready")
    rows_ready = sem("rows_ready")
    scattered = sem("scattered")
    slots_free = sem("slots_free")
    base_ready = sem("base_ready")
    base_stored = sem("base_stored")
    const_ready = sem("const_ready")
    pool_step = sem("pool_step")
    pads_stored = sem("pads_stored")
    passed = sem("passed")

    block = ctx.enter_context(nc.Block())

    x_v = t["x"].rearrange("(b i p) d -> b p i d", b=B, p=P)
    out_v = t["out"][0:T, :].rearrange("(b i p) d -> b i p d", b=B, p=P)
    x2_v = x2_rows[0:T, :].rearrange("(b i p) d -> b i p d", b=B, p=P)
    source = {
        "wq": t["wqT"], "wk": t["wkT"], "wv": t["wvT"], "wo": t["woT"], "gate": t["gateT"],
        "sg": t["sgT"], "su": t["suT"], "sd": t["sdT"],
    }
    ctx_v = t["ctx"].rearrange("(b i p) d -> b p i d", b=B, p=P)

    def slot_of(pair_, name):
        n = WIDTH.get(name, C * D)
        return pair_[:, WSLOT[name], 0:n]

    def weight(name, inner):
        return tuple(slot_of(h, name).rearrange("p (c n) -> p c n", n=inner) for h in (w_hi, w_lo))

    def item_dest(name):
        if name == "ctxT":
            return tuple(h[:, :, :].rearrange("p c n -> p (c n)") for h in ctxT)
        if name == "ctx":
            return tuple(h[:, :, :].rearrange("p c n -> p (c n)") for h in cx)
        return slot_of(w_hi, name), slot_of(w_lo, name)

    def item_stage(name):
        return stage[:, ITEM_AT[name] % 2, 0:WIDTH.get(name, C * D)]

    def split_dest(group):
        kind, n = group
        if kind in ("xnT", "x2T"):
            return tuple(h[:, :, n * P:(n + 1) * P] for h in (xnT if kind == "xnT" else x2T))
        if kind == "pT":
            i, c = n // 2, (n % 2) * 4
            return tuple(h[:, c:c + 4, i * P:(i + 1) * P] for h in pT)
        to = {"q": qT, "k": kT, "v": v, "av": qT}[kind]
        return tuple(h[:, n:n + 1, :] for h in to)

    def bank_of(group):
        return bank[:, AT[group] % BANKS, :]

    def split_source(group):
        kind = group[0]
        inner = P if kind in ("xnT", "x2T", "pT") else 512
        return bank_of(group).rearrange("p (c n) -> p c n", n=inner)

    @block.sync
    def _(sp):
        def load_item(b, name):
            n = ITEM_AT[name]
            sp.wait_ge(item_low, b * NI + n + 1)
            if name == "ctxT":
                src = t["ctxT"][b]
            elif name == "ctx":
                src = ctx_v[b]
            else:
                src = source[name]
            dst = item_stage(name)
            if name == "ctx":
                dst = dst.rearrange("p (c n) -> p c n", n=D)
            sp.dma_start(dst, src).then_inc(stage_loaded[n % 2], 16)

        def body(b, more):
            for name in ("ctxT", "wv", "ctx", "wo"):
                load_item(b, name)
            sp.wait_ge(base_stored, b * 16 * NT + 16 * NT)
            sp.dma_start(res[:, :, :], x_v[b]).then_inc(res_loaded, 16)
            if more:
                sp.wait_ge(group_full, b * PER + AT["xnT", NT - 1] + 1)
                sp.dma_start(xn[:, :, :], x_v[b + 1]).then_inc(x_loaded, 16)
            for name in ("gate", "sg", "su"):
                load_item(b, name)
            for i in range(NT):
                sp.wait_ge(x2_ready, b * NT + i + 1)
                sp.dma_start(x2_v[b, i], x2[:, i, :]).then_inc(x2_stored, 16)
            load_item(b, "sd")
            if more:
                load_item(b + 1, "wq")
                load_item(b + 1, "wk")
            for i in range(NT):
                sp.wait_ge(base_ready, b * NT + i + 1)
                sp.dma_start(out_v[b, i], res[:, i, :]).then_inc(base_stored, 16)

        sp.nop().then_inc(base_stored, 16 * NT)
        sp.dma_start(xn[:, :, :], x_v[0]).then_inc(x_loaded, 16)
        load_item(0, "wq")
        load_item(0, "wk")
        sp.wait_ge(const_ready, 1)
        pad_rows = pbuf[:, 0, 0:2 * E]
        zero_rows = pbuf[:, 1, 0:D]
        sp.dma_start(table.rearrange("(s e) b -> s (e b)", s=CAP), pad_rows).then_inc(pads_stored, 16)
        sp.dma_start(x2_rows[T:ROWS, :], zero_rows).then_inc(pads_stored, 16)
        sp.dma_start(t["out"][T:ROWS, :], zero_rows).then_inc(pads_stored, 16)
        with sp.Fori(0, B - 1) as b:
            body(b, True)
        body(B - 1, False)
        sp.wait_ge(base_stored, 16 * NT * (B + 1))
        sp.wait_ge(x2_stored, 16 * NT * B)
        sp.wait_ge(pads_stored, 48)

    @block.gpsimd
    def _(pool):
        steps = [0]

        def link(ins):
            steps[0] += 1
            ins.then_inc(pool_step, 1)
            pool.wait_ge(pool_step, steps[0])

        pool.memset(pbuf[:, 0, 0:2 * E], 0.0)
        pool.memset(pbuf[:, 1, 0:D], 0.0)
        link(pool.memset(ident[:, :], 0.0))
        pads = pbuf[:, 0, 0:2 * E].rearrange("p (e b) -> p e b", b=2)
        link(pool.iota(pads[:, :, 0], [[0, E]], base=T, channel_multiplier=1,
                       allow_small_or_imprecise_dtypes=True))
        pool.nop().then_inc(const_ready, 1)
        pool.affine_select(out=ident[:, :], in_=ident[:, :], compare_op=ALU.not_equal, fill=1.0,
                           base=0, pattern=[[-1, P]], channel_multiplier=1)
        pool.memset(half[:, :], -0.5)
        pool.memset(ones[:, :], 1.0)
        link(pool.memset(before[:, :], 1.0))
        pool.affine_select(out=before[:, :], in_=before[:, :], compare_op=ALU.is_ge, fill=0.0,
                           base=-1, pattern=[[1, P]], channel_multiplier=-1)
        pool.iota(iota_e[:, :], [[1, E]], base=0, channel_multiplier=0,
                  allow_small_or_imprecise_dtypes=True)
        pool.iota(tok[:, :], [[P, NT]], base=0, channel_multiplier=1,
                  allow_small_or_imprecise_dtypes=True)
        link(pool.memset(earlier[:, 0, :], 0.0))
        pool.nop().then_inc(const_ready, 1)
        pool.nop().then_inc(item_low, 2)
        pool.nop().then_inc(slots_free, 1)

        def low(b, name):
            pool.wait_ge(item_high, b * NI + ITEM_AT[name] + 1)
            hi, lo = item_dest(name)
            pool.tensor_tensor(lo, item_stage(name), hi.bitcast(F32), ALU.subtract).then_inc(item_low, 1)

        def body(b, more):
            for name in ("wk", "ctxT", "wv", "ctx", "wo"):
                low(b, name)
            if more:
                pool.wait_ge(var_ready, b * (NT + 1) + 2)
                pool.tensor_tensor(rstd[:, :], veps[:, :], half[:, :], ALU.pow).then_inc(rstd_ready, 1)
            low(b, "gate")
            for i in range(NT):
                pool.wait_ge(var_ready, b * (NT + 1) + 1 + (1 if more else 0) + i + 1)
                pool.tensor_tensor(rstd2[:, i:i + 1], veps2[:, i:i + 1], half[:, 0:1],
                                   ALU.pow).then_inc(rstd_ready, 1)
            low(b, "sg")
            low(b, "su")
            wait_alone(pool, rows_ready, b + 1, passed)
            for i in range(NT):
                for k in range(K):
                    pool.indirect_dma_start(
                        out=table, out_offset=bass.IndirectOffsetOnAxis(ap=slot[:, i, k:k + 1], axis=0),
                        in_=rows[:, i, k, :], in_offset=None, bounds_check=E * CAP - 1,
                        oob_is_err=False).then_inc(scattered, 16)
                if i == 0:
                    low(b, "sd")
                if i == 1 and more:
                    low(b + 1, "wq")
            pool.wait_ge(scattered, (b + 1) * 16 * NT * K)
            pool.sem_inc(slots_free, 1)

        low(0, "wq")
        pool.wait_ge(var_ready, 1)
        pool.tensor_tensor(rstd[:, :], veps[:, :], half[:, :], ALU.pow).then_inc(rstd_ready, 1)
        pool.wait_ge(pads_stored, 48)
        with pool.Fori(0, B - 1) as b:
            body(b, True)
        body(B - 1, False)
        pool.wait_ge(scattered, 16 * NT * K * B)

    @block.scalar
    def _(act):
        def high_item(b, name):
            n = ITEM_AT[name]
            act.wait_ge(stage_loaded[n % 2], (b * (NI // 2) + n // 2 + 1) * 16)
            act.activation(item_dest(name)[0], item_stage(name), ACT.Copy).then_inc(item_high, 1)

        def after(b, group):
            act.wait_ge(group_full, b * PER + AT[group] + 1)

        def high(b, group):
            after(b, group)
            act.activation(split_dest(group)[0], split_source(group), ACT.Copy).then_inc(high_done, 1)

        def body(b, more):
            for i in range(NT):
                high(b, ("xnT", i))
            high_item(b, "wk")
            for m in range(C):
                high(b, ("q", m))
            high_item(b, "ctxT")
            high_item(b, "wv")
            for m in range(C):
                high(b, ("k", m))
            high_item(b, "ctx")
            high_item(b, "wo")
            act.wait_ge(pads_stored, 48)
            for i in range(NT):
                act.wait_ge(negmax_ready, b * NT + i + 1)
                if i >= 2:
                    after(b, ("pT", 2 * (i - 2) + 1))
                act.activation(pbuf[:, i % 2, :], scores[:, i % 2, :], ACT.Exp,
                               bias=negmax[:, i:i + 1], scale=SCALE,
                               accum_out=rowsum[:, i:i + 1]).then_inc(exp_done, 1)
                high(b, ("v", i))
                if i >= 1:
                    high(b, ("pT", 2 * i - 2))
                    high(b, ("pT", 2 * i - 1))
            high_item(b, "gate")
            high(b, ("pT", 2 * NT - 2))
            high(b, ("pT", 2 * NT - 1))
            for m in range(C):
                high(b, ("av", m))
            after(b, ("wo", NT - 1))
            high_item(b, "sg")
            for i in range(NT):
                high(b, ("x2T", i))
            after(b, ("logits", 0))
            high_item(b, "su")
            for i in range(NT):
                act.wait_ge(negtop_ready, b * NT + i + 1)
                if i:
                    act.wait_ge(router_exp, (b * NT + i) * 2)
                act.activation(elogits[:, :], logits[:, i, :], ACT.Exp, bias=negtop[:, i:i + 1],
                               accum_out=esum[:, i:i + 1]).then_inc(router_exp, 1)
                act.activation(e8[:, i, :], top8[:, i, :], ACT.Exp,
                               bias=negtop[:, i:i + 1]).then_inc(router_exp, 1)
            act.wait_ge(x2_stored, (b + 1) * 16 * NT)
            for m in range(SC):
                after(b, ("g", m))
                act.activation(hid[:, m, :], bank_of(("g", m)), ACT.Silu).then_inc(silu_done, 1)
            high_item(b, "sd")
            for m in range(SC):
                act.wait_ge(hid_ready, b * SC + m + 1)
                act.activation(hT[0][:, m, :], hid[:, m, :], ACT.Copy).then_inc(hid_high, 1)
            if more:
                high_item(b + 1, "wq")

        high_item(0, "wq")
        with act.Fori(0, B - 1) as b:
            body(b, True)
        body(B - 1, False)

    @block.vector
    def _(dve):
        LINKS = 60
        first = [0]
        step = [0]
        batch = [None]

        def link(ins, alone=False):
            step[0] += 1
            ins.then_inc(vec_step, 1)
            if batch[0] is None:
                first[0] = step[0]
                dve.wait_ge(vec_step, step[0])
            elif alone:
                wait_alone(dve, vec_step, batch[0] * LINKS + first[0] + step[0], passed)
            else:
                dve.wait_ge(vec_step, batch[0] * LINKS + first[0] + step[0])

        def low(b, group):
            dve.wait_ge(high_done, b * len(SPLIT) + SPLIT_AT[group] + 1)
            hi, lo = split_dest(group)
            dve.tensor_tensor(lo, split_source(group), hi.bitcast(F32),
                              ALU.subtract).then_inc(group_taken, 1)

        def after(b, group):
            dve.wait_ge(group_full, b * PER + AT[group] + 1)

        def layernorm_stats():
            for i in range(NT):
                last = dve.bn_stats(stats[:, i, :], xn[:, i, :])
            link(last, alone=True)
            for i in range(NT):
                last = dve.bn_aggr(mv[:, i, :], stats[:, i, :])
            link(last)
            dve.tensor_scalar(veps[:, :], mv[:, :, 1], EPS, None, ALU.add).then_inc(var_ready, 1)

        def layernorm_apply():
            for i in range(NT):
                dve.tensor_scalar(xn[:, i, :], xn[:, i, :], mv[:, i, 0:1], rstd[:, i:i + 1],
                                  ALU.subtract, ALU.mult).then_inc(xn_ready, 1)

        def body(b, more):
            step[0] = 0
            batch[0] = b
            for i in range(NT):
                low(b, ("xnT", i))
            for m in range(C):
                low(b, ("q", m))
            for m in range(C):
                low(b, ("k", m))
            for i in range(NT):
                dve.wait_ge(scores_full, b * NT + i + 1)
                link(dve.reduce_max(mx[:, i:i + 1], scores[:, i % 2, :], AX.X))
                dve.tensor_scalar(negmax[:, i:i + 1], mx[:, i:i + 1], -SCALE, None,
                                  ALU.mult).then_inc(negmax_ready, 1)
                low(b, ("v", i))
                if i >= 1:
                    low(b, ("pT", 2 * i - 2))
                    low(b, ("pT", 2 * i - 1))
            low(b, ("pT", 2 * NT - 2))
            low(b, ("pT", 2 * NT - 1))
            dve.wait_ge(exp_done, b * NT + NT)
            link(dve.reciprocal(rinv[:, :], rowsum[:, :]))
            if more:
                dve.wait_ge(x_loaded, (b + 2) * 16)
                layernorm_stats()
            low(b, ("av", 0))
            if more:
                dve.wait_ge(rstd_ready, b * (NT + 1) + 2)
                layernorm_apply()
            for m in range(1, C):
                low(b, ("av", m))
            dve.wait_ge(res_loaded, (b + 1) * 16)

            def second_norm(i):
                dve.wait_ge(rstd_ready, b * (NT + 1) + 1 + (1 if more else 0) + i + 1)
                dve.tensor_scalar(x2[:, i, :], res[:, i, :], mv2[:, i, 0:1], rstd2[:, i:i + 1],
                                  ALU.subtract, ALU.mult).then_inc(x2_ready, 1)

            for i in range(NT):
                after(b, ("wo", i))
                ins = dve.scalar_tensor_tensor(out=res[:, i, :], in0=bank_of(("wo", i)),
                                               scalar=rinv[:, i:i + 1], in1=res[:, i, :],
                                               op0=ALU.mult, op1=ALU.add)
                link(ins)
                dve.nop().then_inc(group_taken, 1)
                link(dve.bn_stats(stats2[:, i, :], res[:, i, :]), alone=True)
                link(dve.bn_aggr(mv2[:, i, :], stats2[:, i, :]))
                dve.tensor_scalar(veps2[:, i:i + 1], mv2[:, i, 1:2], EPS, None,
                                  ALU.add).then_inc(var_ready, 1)
                if i:
                    second_norm(i - 1)
            second_norm(NT - 1)
            for i in range(NT):
                low(b, ("x2T", i))

            after(b, ("logits", 0))
            link(dve.tensor_copy(logits[:, :, :].rearrange("p i e -> p (i e)"),
                                 bank_of(("logits", 0))[:, 0:NT * E]))
            dve.nop().then_inc(group_taken, 1)
            for i in range(NT):
                link(dve.max(top8[:, i, :], logits[:, i, :]))
                dve.tensor_scalar(negtop[:, i:i + 1], top8[:, i, 0:1], -1.0, None,
                                  ALU.mult).then_inc(negtop_ready, 1)
                link(dve.max_index(arg8[:, i, :], top8[:, i, :], logits[:, i, :]))
                link(dve.tensor_copy(argf[:, i, :], arg8[:, i, :]))
                link(dve.tensor_tensor(
                    hot[:, :, :], iota_e[:, :].unsqueeze(1).to_broadcast([P, K, E]),
                    argf[:, i, 0:K].unsqueeze(2).to_broadcast([P, K, E]), ALU.is_equal))
                link(dve.tensor_reduce(chosen[:, :], hot[:, :, :].rearrange("p k e -> p e k"),
                                       AX.X, ALU.add))
                dve.tensor_copy(chosen_b[:, i, :], chosen[:, :])
                link(dve.tensor_tensor(earlier[:, i + 1, :], earlier[:, i, :], chosen[:, :], ALU.add))
                dve.nop().then_inc(chosen_ready, 1)
            dve.wait_ge(silu_done, b * SC + SC)
            dve.nop().then_inc(group_taken, SC)
            after(b, ("pos", 0))
            for i in range(NT):
                for k in range(K):
                    last = dve.scalar_tensor_tensor(
                        out=hot[:, k, :], in0=iota_e[:, :], scalar=argf[:, i, k:k + 1],
                        in1=bank_of(("pos", 0))[:, i * E:(i + 1) * E], op0=ALU.is_equal,
                        op1=ALU.mult, accum_out=posk[:, i, k:k + 1])
                link(last)
            dve.nop().then_inc(group_taken, 1)
            dve.tensor_scalar(over[:, :, :], posk[:, :, :], float(CAP), OVER, ALU.is_ge, ALU.mult)
            link(dve.scalar_tensor_tensor(out=slotf[:, :, :], in0=posk[:, :, :], scalar=float(E),
                                          in1=argf[:, :, 0:K], op0=ALU.mult, op1=ALU.add))
            link(dve.tensor_tensor(slotf[:, :, :], slotf[:, :, :], over[:, :, :], ALU.add))
            dve.wait_ge(router_exp, (b + 1) * 2 * NT)
            link(dve.reciprocal(einv[:, :], esum[:, :]))
            dve.wait_ge(slots_free, b + 1)
            dve.tensor_copy(slot[:, :, :], slotf[:, :, :])
            dve.tensor_copy(rows[:, :, :, 0], tok[:, :].unsqueeze(2).to_broadcast([P, NT, K]))
            link(dve.tensor_tensor(rows[:, :, :, 1], e8[:, :, 0:K],
                                   einv[:, :].unsqueeze(2).to_broadcast([P, NT, K]), ALU.mult))
            dve.nop().then_inc(rows_ready, 1)
            dve.tensor_copy(earlier[:, 0, :], earlier[:, NT, :])
            link(dve.tensor_scalar(tok[:, :], tok[:, :], float(S), None, ALU.add))

            for m in range(SC):
                after(b, ("u", m))
                dve.wait_ge(silu_done, b * SC + m + 1)
                link(dve.tensor_tensor(hid[:, m, :], hid[:, m, :], bank_of(("u", m)), ALU.mult))
                dve.nop().then_inc(group_taken, 1)
                dve.nop().then_inc(hid_ready, 1)
                dve.wait_ge(hid_high, b * SC + m + 1)
                dve.tensor_tensor(hT[1][:, m, :], hid[:, m, :], hT[0][:, m, :].bitcast(F32),
                                  ALU.subtract).then_inc(hT_ready, 1)
            for i in range(NT):
                after(b, ("down", i))
                link(dve.tensor_tensor(res[:, i, :], res[:, i, :], bank_of(("down", i)), ALU.add))
                dve.nop().then_inc(group_taken, 1)
                dve.nop().then_inc(base_ready, 1)

            assert step[0] == (LINKS if more else LINKS - 2), step[0]

        dve.wait_ge(const_ready, 2)
        dve.nop().then_inc(group_taken, BANKS)
        dve.wait_ge(x_loaded, 16)
        layernorm_stats()
        dve.wait_ge(rstd_ready, 1)
        layernorm_apply()
        with dve.Fori(0, B - 1) as b:
            body(b, True)
        body(B - 1, False)

    @block.tensor
    def _(pe):
        def product(out, still, moving, first, last):
            pe.matmul(out, still[0], moving[0], start=first, stop=False)
            pe.matmul(out, still[0], moving[1], start=False, stop=False)
            return pe.matmul(out, still[1], moving[0], start=False, stop=last)

        def at(operand, *index):
            return tuple(h[index] for h in operand)

        def claim(b, group):
            pe.wait_ge(group_taken, b * PER + AT[group] + 1)

        def taken(b, group):
            pe.wait_ge(group_taken, b * PER + AT[group] + 1 + BANKS)

        def item(b, name):
            pe.wait_ge(item_low, b * NI + ITEM_AT[name] + 1 + 2)

        def cols(n, width=P):
            return slice(n * width, (n + 1) * width)

        ALL = slice(None)

        def body(b):
            def chain(group, terms):
                for n, (still, moving) in enumerate(terms):
                    last = product(bank_of(group), still, moving, n == 0, n == len(terms) - 1)
                last.then_inc(group_full, 1)

            def transposes(group, source):
                for j in range(4):
                    last = pe.transpose(bank_of(group)[:, cols(j)], source[:, cols(j)], ident[:, :])
                last.then_inc(group_full, 1)

            for i in range(NT):
                pe.wait_ge(xn_ready, b * NT + i + 1)
                claim(b, ("xnT", i))
                transposes(("xnT", i), xn[:, i, :])
            taken(b, ("xnT", NT - 1))
            for name, kind in (("wq", "q"), ("wk", "k")):
                item(b, name)
                w = weight(name, D)
                for m in range(C):
                    claim(b, (kind, m))
                    chain((kind, m), [(at(w, ALL, c, cols(m)), at(xnT, ALL, c, ALL)) for c in range(C)])

            taken(b, ("k", C - 1))
            item(b, "wv")
            wv = weight("wv", D)

            def scores_of(i):
                if i >= 2:
                    pe.wait_ge(exp_done, b * NT + i - 1)
                for half_, keys in ((0, ctxT), (1, kT)):
                    for c in range(C):
                        last = product(scores[:, i % 2, cols(half_, S)], at(qT, ALL, c, cols(i)),
                                       at(keys, ALL, c, ALL), c == 0, c == C - 1)
                last.then_inc(scores_full, 1)

            def v_of(i):
                claim(b, ("v", i))
                chain(("v", i), [(at(xnT, ALL, c, cols(i)), at(wv, ALL, c, ALL)) for c in range(C)])

            def pT_of(i):
                pe.wait_ge(exp_done, b * NT + i + 1)
                for n in (2 * i, 2 * i + 1):
                    claim(b, ("pT", n))
                    transposes(("pT", n), pbuf[:, i % 2, cols(n % 2, 512)])

            for i in range(NT):
                scores_of(i)
                v_of(i)
                if i >= 1:
                    pT_of(i - 1)
            pT_of(NT - 1)

            taken(b, ("pT", 2 * NT - 1))
            item(b, "ctx")
            for m in range(C):
                claim(b, ("av", m))
                chain(("av", m), [(at(cx if c < C else v, ALL, c % C, cols(m)), at(pT, ALL, c, ALL))
                                  for c in range(2 * C)])
            taken(b, ("av", C - 1))
            item(b, "wo")
            wo = weight("wo", D)
            for i in range(NT):
                claim(b, ("wo", i))
                chain(("wo", i), [(at(qT, ALL, c, cols(i)), at(wo, ALL, c, ALL)) for c in range(C)])

            for i in range(NT):
                pe.wait_ge(x2_ready, b * NT + i + 1)
                claim(b, ("x2T", i))
                transposes(("x2T", i), x2[:, i, :])
            taken(b, ("x2T", NT - 1))
            item(b, "gate")
            gate = weight("gate", E)
            claim(b, ("logits", 0))
            for i in range(NT):
                for c in range(C):
                    last = product(bank_of(("logits", 0))[:, cols(i, E)], at(x2T, ALL, c, cols(i)),
                                   at(gate, ALL, c, ALL), c == 0, c == C - 1)
            last.then_inc(group_full, 1)

            def hidden(name, kind):
                item(b, name)
                w = weight(name, SI)
                for m in range(SC):
                    claim(b, (kind, m))
                    chain((kind, m), [(at(w, ALL, c, cols(m)), at(x2T, ALL, c, ALL)) for c in range(C)])

            hidden("sg", "g")
            pe.wait_ge(chosen_ready, (b + 1) * NT)
            claim(b, ("pos", 0))
            for i in range(NT):
                pos = bank_of(("pos", 0))[:, cols(i, E)]
                pe.matmul(pos, before[:, :], chosen_b[:, i, :], start=True, stop=False)
                last = pe.matmul(pos, ones[:, :], earlier[:, i, :], start=False, stop=True)
            last.then_inc(group_full, 1)
            hidden("su", "u")
            pe.wait_ge(hT_ready, (b + 1) * SC)
            item(b, "sd")
            sd = weight("sd", D)
            for i in range(NT):
                claim(b, ("down", i))
                chain(("down", i), [(at(hT, ALL, m, cols(i)), at(sd, ALL, m, ALL)) for m in range(SC)])

        pe.wait_ge(const_ready, 2)
        with pe.Fori(0, B) as b:
            body(b)


def routed_experts(nc, ctx, t, table, x2_rows):
    def sb(name, shape, dt=F32):
        return ctx.enter_context(nc.sbuf_tensor(name, shape, dt))

    def sem(name):
        return ctx.enter_context(nc.semaphore(name))

    U = 4
    LAST = E // U - 1
    gu = sb("gu", [P, U, C * 2 * I])
    dn = sb("dn", [P, U, 2 * D])
    tab = sb("tab", [P, E, 2])
    idx_all = sb("idx_all", [P, E], I32)
    idx = sb("idx", [P, U], I32)
    xg = sb("xg", [P, U, D])
    xgT = sb("xgT", [P, 2, D])
    silu = sb("silu", [P, 2, I])
    hid = sb("hid_e", [P, 2, 2 * P])
    hidT = sb("hidT", [P, 2, 2 * P])
    eo = sb("eo", [P, U, D])
    ident = sb("ident_e", [P, P])

    ps_xgT = ctx.enter_context(nc.psum_tensor("ps_xgT", [P, 2, 512], F32))
    ps_gu = ctx.enter_context(nc.psum_tensor("ps_gu", [P, 2, 512], F32))
    ps_hidT = ctx.enter_context(nc.psum_tensor("ps_hidT", [P, 2, 512], F32))
    ps_dn = ctx.enter_context(nc.psum_tensor("ps_dn", [P, 2, 512], F32))

    weights_loaded = [sem(f"weights_loaded{u}") for u in range(U)]
    gathered = [sem(f"gathered{u}") for u in range(U)]
    tab_loaded = sem("tab_loaded")
    idx_ready = sem("idx_ready")
    zero_ready = sem("zero_ready")
    ident_step = sem("ident_step")
    idx_copied = sem("idx_copied")
    xgT_full = sem("xgT_full")
    xgT_copied = sem("xgT_copied")
    gu_full = sem("gu_full")
    silu_ready = sem("silu_ready")
    hid_made = sem("hid_made")
    hidT_full = sem("hidT_full")
    hidT_copied = sem("hidT_copied")
    dn_full = sem("dn_full")
    eo_ready = sem("eo_ready")
    added = sem("added")
    rows_added = sem("rows_added")
    passed = sem("passed_e")

    block = ctx.enter_context(nc.Block())

    def run(eng, step):
        with eng.Fori(0, LAST) as j:
            for u in range(U):
                step(j, u, U)
        for u in range(U):
            step(LAST, u, U - 1 - u)

    @block.sync
    def _(sp):
        def load(j, u):
            e = j * U + u
            guv = t["gate_up"][e].rearrange("(c p) n -> p c n", p=P)
            sp.dma_start(gu[:, u, :].rearrange("p (c n) -> p c n", n=2 * I), guv).then_inc(weights_loaded[u], 16)
            sp.dma_start(dn[:, u, 0:D], t["down"][e, 0:P, :]).then_inc(weights_loaded[u], 16)
            sp.dma_start(dn[0:I - P, u, D:2 * D], t["down"][e, P:I, :]).then_inc(weights_loaded[u], 16)

        sp.dma_start(tab[:, :, :].rearrange("p e b -> p (e b)"),
                     table.rearrange("(s e) b -> s (e b)", s=CAP)).then_inc(tab_loaded, 16)
        sp.wait_ge(zero_ready, 1)
        for u in range(U):
            load(0, u)

        def step(j, u, behind):
            if behind >= U:
                sp.wait_ge(dn_full, j * U + u + 1)
                load(j + 1, u)
        run(sp, step)

    @block.gpsimd
    def _(pool):
        pool.memset(ident[:, :], 0.0).then_inc(ident_step, 1)
        pool.wait_ge(ident_step, 1)
        pool.affine_select(out=ident[:, :], in_=ident[:, :], compare_op=ALU.not_equal, fill=1.0,
                           base=0, pattern=[[-1, P]], channel_multiplier=1).then_inc(ident_step, 1)
        pool.nop().then_inc(rows_added, U)

        def gather(e, u):
            pool.tensor_copy(idx[:, u:u + 1], idx_all[:, bass.ds(e, 1)]).then_inc(idx_copied, 1)
            wait_alone(pool, idx_copied, e + 1, passed)
            pool.indirect_dma_start(
                out=xg[:, u, :], out_offset=None, in_=x2_rows,
                in_offset=bass.IndirectOffsetOnAxis(ap=idx[:, u:u + 1], axis=0)).then_inc(gathered[u], 16)

        pool.wait_ge(idx_ready, 1)
        for u in range(U):
            gather(u, u)

        def step(j, u, behind):
            e = j * U + u
            wait_alone(pool, eo_ready, e + 1 + 2, passed)
            pool.indirect_dma_start(
                out=t["out"], out_offset=bass.IndirectOffsetOnAxis(ap=idx[:, u:u + 1], axis=0),
                in_=eo[:, u, :], in_offset=None, compute_op=ALU.add).then_inc(added, 16)
            pool.wait_ge(added, (e + 1) * 16)
            pool.sem_inc(rows_added, 1)
            if behind >= U:
                wait_alone(pool, xgT_full, e + 1, passed)
                gather(e + U, u)
        run(pool, step)

    @block.scalar
    def _(act):
        def copy_xgT(e, s):
            act.wait_ge(xgT_full, e + 1)
            act.activation(xgT[:, s, :], ps_xgT[:, s, :], ACT.Copy).then_inc(xgT_copied, 1)

        def gate(e, s):
            act.wait_ge(gu_full, e + 1)
            act.activation(silu[:, s, :], ps_gu[:, s, 0:I], ACT.Silu).then_inc(silu_ready, 1)

        copy_xgT(0, 0)
        copy_xgT(1, 1)
        gate(0, 0)

        def step(j, u, behind):
            e = j * U + u
            if behind >= 2:
                copy_xgT(e + 2, u % 2)
            if behind >= 1:
                gate(e + 1, (u + 1) % 2)
        run(act, step)

    @block.vector
    def _(dve):
        dve.memset(hid[:, :, :], 0.0)
        dve.memset(dn[:, :, :], 0.0).then_inc(zero_ready, 1)
        dve.wait_ge(zero_ready, 1)
        dve.nop().then_inc(eo_ready, 2)
        dve.wait_ge(tab_loaded, 16)
        dve.tensor_copy(idx_all[:, :], tab[:, :, 0]).then_inc(idx_ready, 1)

        def up(e, s):
            dve.wait_ge(silu_ready, e + 1)
            dve.tensor_tensor(hid[:, s, 0:I], silu[:, s, :], ps_gu[:, s, I:2 * I],
                              ALU.mult).then_inc(hid_made, 1)

        up(0, 0)

        def step(j, u, behind):
            e = j * U + u
            s = u % 2
            dve.wait_ge(hidT_full, e + 1)
            dve.tensor_copy(hidT[:, s, :], ps_hidT[:, s, 0:2 * P]).then_inc(hidT_copied, 1)
            if behind >= 1:
                up(e + 1, (u + 1) % 2)
            dve.wait_ge(dn_full, e + 1)
            dve.wait_ge(rows_added, e + 1)
            dve.tensor_scalar(eo[:, u, :], ps_dn[:, s, :], tab[:, bass.ds(e, 1), 1], None,
                              ALU.mult).then_inc(eo_ready, 1)
        run(dve, step)

    @block.tensor
    def _(pe):
        def transpose_rows(j, u, s):
            pe.wait_ge(gathered[u], (j + 1) * 16)
            for c in range(C):
                last = pe.transpose(ps_xgT[:, s, c * P:(c + 1) * P], xg[:, u, c * P:(c + 1) * P], ident[:, :])
            last.then_inc(xgT_full, 1)

        def gate_up(j, u):
            e = j * U + u
            pe.wait_ge(xgT_copied, e + 1)
            pe.wait_ge(weights_loaded[u], (j + 1) * 48)
            for c in range(C):
                last = pe.matmul(ps_gu[:, u % 2, 0:2 * I], xgT[:, u % 2, c * P:(c + 1) * P],
                                 gu[:, u, c * 2 * I:(c + 1) * 2 * I], start=c == 0, stop=c == C - 1)
            last.then_inc(gu_full, 1)

        pe.wait_ge(ident_step, 2)
        transpose_rows(0, 0, 0)
        transpose_rows(0, 1, 1)
        gate_up(0, 0)

        def step(j, u, behind):
            e = j * U + u
            s = u % 2
            pe.wait_ge(hid_made, e + 1)
            for c in range(2):
                last = pe.transpose(ps_hidT[:, s, c * P:(c + 1) * P], hid[:, s, c * P:(c + 1) * P], ident[:, :])
            last.then_inc(hidT_full, 1)
            if behind >= 2:
                transpose_rows(j + (u + 2) // U, (u + 2) % U, s)
            if behind >= 1:
                gate_up(j + (u + 1) // U, (u + 1) % U)
            pe.wait_ge(hidT_copied, e + 1)
            pe.wait_ge(eo_ready, e + 1)
            for c in range(2):
                last = pe.matmul(ps_dn[:, s, :], hidT[:, s, c * P:(c + 1) * P],
                                 dn[:, u, c * D:(c + 1) * D], start=c == 0, stop=c == 1)
            last.then_inc(dn_full, 1)
        run(pe, step)


def build(nc, t):
    table = nc.dram_tensor("table", (E * CAP, 2), F32, kind="Internal").ap()
    x2_rows = nc.dram_tensor("x2_rows", (ROWS, D), F32, kind="Internal").ap()
    with ExitStack() as ctx:
        attention_and_shared(nc, ctx, t, table, x2_rows)
    with ExitStack() as ctx:
        routed_experts(nc, ctx, t, table, x2_rows)


def kernel(x, ctx_2048, mask_BxSx4224_bf0, L0_xattn_wq, L0_xattn_wk, L0_xattn_wv, L0_xattn_wo,
           L0_ffn_gate_w, L0_ffn_gate_up_proj, L0_ffn_down_proj, L0_ffn_shared_gate_w,
           L0_ffn_shared_up_w, L0_ffn_shared_down_w):
    import concourse.bacc as bacc
    from concourse.bass_utils import run_bass_kernel_spmd

    def chunked(w):
        n = w.shape[1]
        return np.ascontiguousarray(w.reshape(-1, P, n).transpose(1, 0, 2).reshape(P, -1))

    def arr(a):
        return np.asarray(a)

    context = arr(ctx_2048)
    arrays = {
        "x": np.ascontiguousarray(arr(x).reshape(T, D)),
        "ctx": np.ascontiguousarray(context.reshape(T, D)),
        "ctxT": np.stack([chunked(context[b].T) for b in range(B)]),
        "wqT": chunked(arr(L0_xattn_wq).T),
        "wkT": chunked(arr(L0_xattn_wk).T),
        "wvT": chunked(arr(L0_xattn_wv).T),
        "woT": chunked(arr(L0_xattn_wo).T),
        "gateT": chunked(arr(L0_ffn_gate_w).T),
        "sgT": chunked(arr(L0_ffn_shared_gate_w).T),
        "suT": chunked(arr(L0_ffn_shared_up_w).T),
        "sdT": chunked(arr(L0_ffn_shared_down_w).T),
        "gate_up": np.ascontiguousarray(arr(L0_ffn_gate_up_proj)),
        "down": np.ascontiguousarray(arr(L0_ffn_down_proj)),
    }
    nc = bacc.Bacc("TRN2", target_bir_lowering=False, num_devices=1)
    t = {name: nc.dram_tensor(name + "_in", a.shape, mybir.dt.from_np(a.dtype), kind="ExternalInput").ap()
         for name, a in arrays.items()}
    t["out"] = nc.dram_tensor("out_rows", (ROWS, D), F32, kind="ExternalOutput").ap()
    build(nc, t)
    r = run_bass_kernel_spmd(nc, [{name + "_in": a for name, a in arrays.items()}], core_ids=[0])
    return r.results[0]["out_rows"][0:T].reshape(B, S, D)
```

```python
from contextlib import ExitStack

import numpy as np

import concourse.bass as bass
from concourse import mybir

F32 = mybir.dt.float32
F32R = mybir.dt.float32r
BF16 = mybir.dt.bfloat16
I32 = mybir.dt.int32
U32 = mybir.dt.uint32
ALU = mybir.AluOpType
ACT = mybir.ActivationFunctionType
AX = mybir.AxisListType

P = 128
B, S, D = 4, 512, 512
T = B * S
C = D // P
NT = S // P
KV = 2 * S
E, K, CAP = 64, 6, 128
I = 192
SI = 2 * I
EPS = 1e-5
SCALE = float(D) ** -0.5
ROWS = T + CAP
OVER = float(1 << 20)

BANKS = 4
FIRST = [("xnT", i) for i in range(NT)] + [("q", m) for m in range(C)] + [("k", m) for m in range(C)]


def groups_of(more):
    nxt = more * 1
    return (
        [("v", 0), ("v", 1), ("pT", 0), ("pT", 1), ("v", 2), ("pT", 2), ("pT", 3), ("v", 3)]
        + [("pT", n) for n in range(4, 2 * NT)]
        + [("xnT", 0), ("xnT", 1)] * nxt + [("av", m) for m in range(C)]
        + [("xnT", 2), ("xnT", 3)] * nxt + [("wo", i) for i in range(NT)]
        + [("q", 0), ("q", 1)] * nxt + [("x2T", i) for i in range(NT)] + [("q", 2), ("q", 3)] * nxt
        + [("logitsT", 0)] + [("k", 0)] * nxt + [("logits", 0)]
        + [("k", 1), ("k", 2), ("k", 3)] * nxt + [("pos", 0), ("pos", 1)]
    )


GROUPS = {"first": FIRST, True: groups_of(True), False: groups_of(False)}
PER = len(GROUPS[True])
assert PER % BANKS == 0 and len(FIRST) % BANKS == 0
AT = {key: {name: n for n, name in enumerate(groups)} for key, groups in GROUPS.items()}
SPLIT = {key: [g for g in groups if g[0] in ("xnT", "q", "k", "v", "pT", "av", "x2T")]
         for key, groups in GROUPS.items()}
SPLIT_AT = {key: {name: n for n, name in enumerate(groups)} for key, groups in SPLIT.items()}
FIRST_ITEMS = ["gate", "wq'", "wk'", "ctxT'", "wv'"]
ITEMS = ["ctx", "wo", "ctxT'", "wq'", "wk'", "wv'"]
WSLOT = {"wq'": 0, "wk'": 1, "wv'": 0, "wo": 1}


def place(b, key, group):
    return AT[key][group] if key == "first" else len(FIRST) + b * PER + AT[key][group]


def split_place(b, key, group):
    if key == "first":
        return SPLIT_AT[key][group]
    return len(SPLIT["first"]) + b * len(SPLIT[True]) + SPLIT_AT[key][group]


def item_place(b, key, name):
    return FIRST_ITEMS.index(name) if key == "first" else len(FIRST_ITEMS) + b * len(ITEMS) + ITEMS.index(name)


def wait_alone(eng, sem, value, passed):
    eng.wait_ge(sem, value)
    eng.sem_inc(passed, 1)


def attention_and_router(nc, ctx, t, table, x2_rows):
    def sb(name, shape, dt=F32):
        return ctx.enter_context(nc.sbuf_tensor(name, shape, dt))

    def sem(name):
        return ctx.enter_context(nc.semaphore(name))

    def pair(name, shape):
        return sb(name + "_hi", shape, F32R), sb(name + "_lo", shape, F32R)

    stage = sb("stage", [P, 2, C * D])
    w = pair("w", [P, 2, C * D])
    gate = pair("gate", [P, C, E])
    xnT = pair("xnT", [P, C, S])
    ctxT = pair("ctxT", [P, C, S])
    cx = pair("cx", [P, C, D])
    qT = pair("qT", [P, C, S])
    kT = pair("kT", [P, C, S])
    v = pair("v", [P, NT, D])
    pT = pair("pT", [P, KV // P, S])
    x2T = tuple(h[:, 0:C, :] for h in pT)
    pbuf = sb("pbuf", [P, 2, KV])
    x2 = pbuf[:, :, :].rearrange("p a (b d) -> p (a b) d", d=D)
    xn = sb("xn", [P, NT, D])
    logitsT = xn[0:E, 0, :]
    hot = xn[:, 1, 0:K * E].rearrange("p (k e) -> p k e", e=E)
    res = sb("res", [P, NT, D])
    ident = sb("ident", [P, P])
    before = sb("before", [P, P], BF16)
    ones = sb("ones", [P, P], BF16)
    iota_e = sb("iota_e", [P, E])
    half = sb("half", [P, NT])
    stats = sb("stats", [P, NT, 6])
    mv = sb("mv", [P, NT, 2])
    veps = sb("veps", [P, NT])
    rstd = sb("rstd", [P, NT])
    stats2 = sb("stats2", [P, NT, 6])
    mv2 = sb("mv2", [P, NT, 2])
    veps2 = sb("veps2", [P, NT])
    rstd2 = sb("rstd2", [P, NT])
    mx = sb("mx", [P, NT])
    negmax = sb("negmax", [P, NT])
    rowsum = sb("rowsum", [P, NT])
    rinv = sb("rinv", [P, NT])
    logits = sb("logits", [P, NT, E])
    top8 = sb("top8", [P, NT, 8])
    arg8 = sb("arg8", [P, NT, 8], U32)
    argf = sb("argf", [P, NT, 8])
    negtop = sb("negtop", [P, NT])
    e8 = sb("e8", [P, NT, 8])
    elogits = sb("elogits", [P, E])
    esum = sb("esum", [P, NT])
    einv = sb("einv", [P, NT])
    chosen = sb("chosen", [P, E])
    chosen_b = sb("chosen_b", [P, NT, E], BF16)
    earlier = sb("earlier", [P, NT + 1, E], BF16)
    posk = sb("posk", [P, NT, K])
    over = sb("over", [P, NT, K])
    slotf = sb("slotf", [P, NT, K])
    slot = sb("slot", [P, NT, K], I32)
    tok = sb("tok", [P, NT])
    rows = sb("rows", [P, NT, K, 2])

    bank = ctx.enter_context(nc.psum_tensor("bank", [P, BANKS, 512], F32))
    scores = ctx.enter_context(nc.psum_tensor("scores", [P, 2, KV], F32))

    stage_loaded = [sem("stage_loaded0"), sem("stage_loaded1")]
    item_high = sem("item_high")
    item_low = sem("item_low")
    x_loaded = sem("x_loaded")
    res_loaded = sem("res_loaded")
    group_full = sem("group_full")
    group_taken = sem("group_taken")
    high_done = sem("high_done")
    vec_step = sem("vec_step")
    xn_ready = sem("xn_ready")
    scores_full = sem("scores_full")
    negmax_ready = sem("negmax_ready")
    exp_done = sem("exp_done")
    var_ready = sem("var_ready")
    rstd_ready = sem("rstd_ready")
    x2_ready = sem("x2_ready")
    x2_stored = sem("x2_stored")
    logitsT_ready = sem("logitsT_ready")
    negtop_ready = sem("negtop_ready")
    router_exp = sem("router_exp")
    chosen_ready = sem("chosen_ready")
    rows_ready = sem("rows_ready")
    scattered = sem("scattered")
    slots_free = sem("slots_free")
    base_ready = sem("base_ready")
    base_stored = sem("base_stored")
    const_ready = sem("const_ready")
    pool_step = sem("pool_step")
    pads_stored = sem("pads_stored")
    passed = sem("passed")

    block = ctx.enter_context(nc.Block())

    x_v = t["x"].rearrange("(b i p) d -> b p i d", b=B, p=P)
    out_v = t["out"][0:T, :].rearrange("(b i p) d -> b i p d", b=B, p=P)
    x2_v = x2_rows[0:T, :].rearrange("(b i p) d -> b i p d", b=B, p=P)
    ctx_v = t["ctx"].rearrange("(b i p) d -> b p i d", b=B, p=P)
    weight_source = {"wq'": t["wqT"], "wk'": t["wkT"], "wv'": t["wvT"], "wo": t["woT"]}

    def flat(operand):
        return tuple(h[:, :, :].rearrange("p c n -> p (c n)") for h in operand)

    def weight(name):
        return tuple(h[:, WSLOT[name], :].rearrange("p (c n) -> p c n", n=D) for h in w)

    def item_dest(name):
        if name in WSLOT:
            return tuple(h[:, WSLOT[name], :] for h in w)
        return flat({"ctxT'": ctxT, "ctx": cx, "gate": gate}[name])

    def item_stage(b, key, name):
        parity = (FIRST_ITEMS.index(name) if key == "first"
                  else len(FIRST_ITEMS) + ITEMS.index(name)) % 2
        return stage[:, parity, 0:(C * E if name == "gate" else C * D)]

    def split_dest(group):
        kind, n = group
        if kind in ("xnT", "x2T"):
            return tuple(h[:, :, n * P:(n + 1) * P] for h in (xnT if kind == "xnT" else x2T))
        if kind == "pT":
            i, c = n // 2, (n % 2) * 4
            return tuple(h[:, c:c + 4, i * P:(i + 1) * P] for h in pT)
        to = {"q": qT, "k": kT, "v": v, "av": qT}[kind]
        return tuple(h[:, n:n + 1, :] for h in to)

    def bank_of(key, group):
        return bank[:, AT[key][group] % BANKS, :]

    def split_source(key, group):
        inner = P if group[0] in ("xnT", "x2T", "pT") else 512
        return bank_of(key, group).rearrange("p (c n) -> p c n", n=inner)

    @block.sync
    def _(sp):
        def load_item(b, key, name, source_batch=None):
            n = item_place(b, key, name)
            sp.wait_ge(item_low, n + 1)
            dst = item_stage(b, key, name)
            if name == "gate":
                src = t["gateT"]
            elif name == "ctxT'":
                src = t["ctxT"][source_batch]
            elif name == "ctx":
                dst = dst.rearrange("p (c n) -> p c n", n=D)
                src = ctx_v[source_batch]
            else:
                src = weight_source[name]
            parity = (FIRST_ITEMS.index(name) if key == "first"
                      else len(FIRST_ITEMS) + ITEMS.index(name)) % 2
            sp.dma_start(dst, src).then_inc(stage_loaded[parity], 16)

        def body(b, more):
            load_item(b, more, "ctx", b)
            load_item(b, more, "wo")
            if more:
                sp.wait_ge(group_taken, b * PER + len(FIRST) + BANKS)
                sp.dma_start(xn[:, :, :], x_v[b + 1]).then_inc(x_loaded, 16)
            sp.wait_ge(base_stored, b * 16 * NT + 16 * NT)
            sp.dma_start(res[:, :, :], x_v[b]).then_inc(res_loaded, 16)
            if more:
                for name in ("ctxT'", "wq'", "wk'"):
                    load_item(b, more, name, b + 1)
            for i in range(NT):
                sp.wait_ge(base_ready, b * NT + i + 1)
                sp.dma_start(out_v[b, i], res[:, i, :]).then_inc(base_stored, 16)
                sp.wait_ge(x2_ready, b * NT + i + 1)
                sp.dma_start(x2_v[b, i], x2[:, i, :]).then_inc(x2_stored, 16)
            if more:
                load_item(b, more, "wv'")

        sp.nop().then_inc(base_stored, 16 * NT)
        sp.dma_start(xn[:, :, :], x_v[0]).then_inc(x_loaded, 16)
        sp.wait_ge(const_ready, 1)
        for name in FIRST_ITEMS:
            load_item(0, "first", name, 0)
        pad_rows = pbuf[:, 0, 0:2 * E]
        zero_rows = pbuf[:, 1, 0:D]
        sp.dma_start(table.rearrange("(s e) b -> s (e b)", s=CAP), pad_rows).then_inc(pads_stored, 16)
        sp.dma_start(x2_rows[T:ROWS, :], zero_rows).then_inc(pads_stored, 16)
        sp.dma_start(t["out"][T:ROWS, :], zero_rows).then_inc(pads_stored, 16)
        with sp.Fori(0, B - 1) as b:
            body(b, True)
        body(B - 1, False)
        sp.wait_ge(base_stored, 16 * NT * (B + 1))
        sp.wait_ge(x2_stored, 16 * NT * B)
        sp.wait_ge(pads_stored, 48)

    @block.gpsimd
    def _(pool):
        steps = [0]

        def link(ins):
            steps[0] += 1
            ins.then_inc(pool_step, 1)
            pool.wait_ge(pool_step, steps[0])

        pool.memset(pbuf[:, 0, 0:2 * E], 0.0)
        pool.memset(pbuf[:, 1, 0:D], 0.0)
        link(pool.memset(ident[:, :], 0.0))
        pads = pbuf[:, 0, 0:2 * E].rearrange("p (e b) -> p e b", b=2)
        link(pool.iota(pads[:, :, 0], [[0, E]], base=T, channel_multiplier=1,
                       allow_small_or_imprecise_dtypes=True))
        pool.nop().then_inc(const_ready, 1)
        pool.affine_select(out=ident[:, :], in_=ident[:, :], compare_op=ALU.not_equal, fill=1.0,
                           base=0, pattern=[[-1, P]], channel_multiplier=1)
        pool.memset(half[:, :], -0.5)
        pool.memset(ones[:, :], 1.0)
        link(pool.memset(before[:, :], 1.0))
        pool.affine_select(out=before[:, :], in_=before[:, :], compare_op=ALU.is_ge, fill=0.0,
                           base=-1, pattern=[[1, P]], channel_multiplier=-1)
        pool.iota(iota_e[:, :], [[1, E]], base=0, channel_multiplier=0,
                  allow_small_or_imprecise_dtypes=True)
        pool.iota(tok[:, :], [[P, NT]], base=0, channel_multiplier=1,
                  allow_small_or_imprecise_dtypes=True)
        link(pool.memset(earlier[:, 0, :], 0.0))
        pool.nop().then_inc(const_ready, 1)
        pool.nop().then_inc(slots_free, 1)

        def body(b, more):
            if more:
                pool.wait_ge(var_ready, b * (NT + 1) + 2)
                pool.tensor_tensor(rstd[:, :], veps[:, :], half[:, :], ALU.pow).then_inc(rstd_ready, 1)
            for i in range(NT):
                pool.wait_ge(var_ready, b * (NT + 1) + 1 + (1 if more else 0) + i + 1)
                pool.tensor_tensor(rstd2[:, i:i + 1], veps2[:, i:i + 1], half[:, 0:1],
                                   ALU.pow).then_inc(rstd_ready, 1)
            wait_alone(pool, rows_ready, b + 1, passed)
            for i in range(NT):
                for k in range(K):
                    pool.indirect_dma_start(
                        out=table, out_offset=bass.IndirectOffsetOnAxis(ap=slot[:, i, k:k + 1], axis=0),
                        in_=rows[:, i, k, :], in_offset=None, bounds_check=E * CAP - 1,
                        oob_is_err=False).then_inc(scattered, 16)
            pool.wait_ge(scattered, (b + 1) * 16 * NT * K)
            pool.sem_inc(slots_free, 1)

        pool.wait_ge(var_ready, 1)
        pool.tensor_tensor(rstd[:, :], veps[:, :], half[:, :], ALU.pow).then_inc(rstd_ready, 1)
        pool.wait_ge(pads_stored, 48)
        with pool.Fori(0, B - 1) as b:
            body(b, True)
        body(B - 1, False)
        pool.wait_ge(scattered, 16 * NT * K * B)

    @block.scalar
    def _(act):
        def high_item(b, key, name):
            n = (FIRST_ITEMS.index(name) if key == "first" else len(FIRST_ITEMS) + ITEMS.index(name))
            loads = n // 2 + 1 if key == "first" else b * (len(ITEMS) // 2) + n // 2 + 1
            act.wait_ge(stage_loaded[n % 2], loads * 16)
            act.activation(item_dest(name)[0], item_stage(b, key, name), ACT.Copy).then_inc(item_high, 1)

        def after(b, key, group):
            act.wait_ge(group_full, place(b, key, group) + 1)

        def high(b, key, group):
            after(b, key, group)
            act.activation(split_dest(group)[0], split_source(key, group), ACT.Copy).then_inc(high_done, 1)

        def body(b, more):
            def exp(i):
                act.wait_ge(negmax_ready, b * NT + i + 1)
                if i >= 2:
                    after(b, more, ("pT", 2 * (i - 2) + 1))
                act.activation(pbuf[:, i % 2, :], scores[:, i % 2, :], ACT.Exp,
                               bias=negmax[:, i:i + 1], scale=SCALE,
                               accum_out=rowsum[:, i:i + 1]).then_inc(exp_done, 1)

            def h(*groups):
                for group in groups:
                    high(b, more, group)

            h(("v", 0))
            high_item(b, more, "ctx")
            exp(0)
            exp(1)
            h(("v", 1), ("pT", 0), ("pT", 1))
            high_item(b, more, "wo")
            exp(2)
            h(("v", 2), ("pT", 2), ("pT", 3))
            exp(3)
            h(("v", 3))
            h(*[("pT", n) for n in range(4, 2 * NT)])
            if more:
                h(("xnT", 0), ("xnT", 1))
                high_item(b, more, "ctxT'")
                high_item(b, more, "wq'")
            h(*[("av", m) for m in range(C)])
            if more:
                h(("xnT", 2), ("xnT", 3))
                after(b, more, ("wo", NT - 1))
                high_item(b, more, "wk'")
                h(("q", 0), ("q", 1))
            h(*[("x2T", i) for i in range(NT)])
            if more:
                h(("q", 2), ("q", 3))
                high_item(b, more, "wv'")
                h(("k", 0))
            for i in range(NT):
                act.wait_ge(negtop_ready, b * NT + i + 1)
                if i:
                    act.wait_ge(router_exp, (b * NT + i) * 2)
                act.activation(elogits[:, :], logits[:, i, :], ACT.Exp, bias=negtop[:, i:i + 1],
                               accum_out=esum[:, i:i + 1]).then_inc(router_exp, 1)
                act.activation(e8[:, i, :], top8[:, i, :], ACT.Exp,
                               bias=negtop[:, i:i + 1]).then_inc(router_exp, 1)
                if more and i < 3:
                    h(("k", i + 1))
            act.wait_ge(x2_stored, (b + 1) * 16 * NT)

        for name in ("gate", "wq'", "wk'"):
            high_item(0, "first", name)
        for i in range(NT):
            high(0, "first", ("xnT", i))
        high_item(0, "first", "ctxT'")
        for m in range(C):
            high(0, "first", ("q", m))
        high_item(0, "first", "wv'")
        for m in range(C):
            high(0, "first", ("k", m))
        act.wait_ge(pads_stored, 48)
        with act.Fori(0, B - 1) as b:
            body(b, True)
        body(B - 1, False)

    @block.vector
    def _(dve):
        LINKS = 54
        first = [0]
        step = [0]
        batch = [None]

        def link(ins, alone=False):
            step[0] += 1
            ins.then_inc(vec_step, 1)
            if batch[0] is None:
                first[0] = step[0]
                dve.wait_ge(vec_step, step[0])
            elif alone:
                wait_alone(dve, vec_step, batch[0] * LINKS + first[0] + step[0], passed)
            else:
                dve.wait_ge(vec_step, batch[0] * LINKS + first[0] + step[0])

        def low_item(b, key, name):
            dve.wait_ge(item_high, item_place(b, key, name) + 1)
            hi, lo = item_dest(name)
            dve.tensor_tensor(lo, item_stage(b, key, name), hi.bitcast(F32),
                              ALU.subtract).then_inc(item_low, 1)

        def low(b, key, group):
            dve.wait_ge(high_done, split_place(b, key, group) + 1)
            hi, lo = split_dest(group)
            dve.tensor_tensor(lo, split_source(key, group), hi.bitcast(F32),
                              ALU.subtract).then_inc(group_taken, 1)

        def layernorm_stats():
            for i in range(NT):
                last = dve.bn_stats(stats[:, i, :], xn[:, i, :])
            link(last, alone=True)
            for i in range(NT):
                last = dve.bn_aggr(mv[:, i, :], stats[:, i, :])
            link(last)
            dve.tensor_scalar(veps[:, :], mv[:, :, 1], EPS, None, ALU.add).then_inc(var_ready, 1)

        def layernorm_apply():
            for i in range(NT):
                dve.tensor_scalar(xn[:, i, :], xn[:, i, :], mv[:, i, 0:1], rstd[:, i:i + 1],
                                  ALU.subtract, ALU.mult).then_inc(xn_ready, 1)

        def body(b, more):
            step[0] = 0
            batch[0] = b

            def after(group):
                dve.wait_ge(group_full, place(b, more, group) + 1)

            def l(*groups):
                for group in groups:
                    low(b, more, group)

            def maximum(i):
                dve.wait_ge(scores_full, b * NT + i + 1)
                link(dve.reduce_max(mx[:, i:i + 1], scores[:, i % 2, :], AX.X))
                dve.tensor_scalar(negmax[:, i:i + 1], mx[:, i:i + 1], -SCALE, None,
                                  ALU.mult).then_inc(negmax_ready, 1)

            def second_norm(i):
                dve.wait_ge(rstd_ready, b * (NT + 1) + 1 + (1 if more else 0) + i + 1)
                dve.tensor_scalar(x2[:, i, :], res[:, i, :], mv2[:, i, 0:1], rstd2[:, i:i + 1],
                                  ALU.subtract, ALU.mult).then_inc(x2_ready, 1)

            l(("v", 0))
            low_item(b, more, "ctx")
            maximum(0)
            maximum(1)
            l(("v", 1), ("pT", 0), ("pT", 1))
            low_item(b, more, "wo")
            maximum(2)
            l(("v", 2), ("pT", 2), ("pT", 3))
            if more:
                dve.wait_ge(x_loaded, (b + 2) * 16)
                layernorm_stats()
            maximum(3)
            l(("v", 3))
            if more:
                dve.wait_ge(rstd_ready, b * (NT + 1) + 2)
                layernorm_apply()
            l(*[("pT", n) for n in range(4, 2 * NT)])
            dve.wait_ge(exp_done, b * NT + NT)
            link(dve.reciprocal(rinv[:, :], rowsum[:, :]))
            if more:
                l(("xnT", 0), ("xnT", 1))
                low_item(b, more, "ctxT'")
                low_item(b, more, "wq'")
            l(*[("av", m) for m in range(C)])
            if more:
                l(("xnT", 2), ("xnT", 3))
            dve.wait_ge(res_loaded, (b + 1) * 16)

            for i in range(NT):
                after(("wo", i))
                link(dve.scalar_tensor_tensor(out=res[:, i, :], in0=bank_of(more, ("wo", i)),
                                              scalar=rinv[:, i:i + 1], in1=res[:, i, :],
                                              op0=ALU.mult, op1=ALU.add))
                dve.nop().then_inc(group_taken, 1)
                dve.nop().then_inc(base_ready, 1)
                link(dve.bn_stats(stats2[:, i, :], res[:, i, :]), alone=True)
                link(dve.bn_aggr(mv2[:, i, :], stats2[:, i, :]))
                dve.tensor_scalar(veps2[:, i:i + 1], mv2[:, i, 1:2], EPS, None,
                                  ALU.add).then_inc(var_ready, 1)
                if i:
                    second_norm(i - 1)
            second_norm(NT - 1)
            if more:
                l(("q", 0), ("q", 1))
                low_item(b, more, "wk'")
            l(*[("x2T", i) for i in range(NT)])
            if more:
                l(("q", 2), ("q", 3))
            after(("logitsT", 0))
            link(dve.tensor_copy(logitsT, bank_of(more, ("logitsT", 0))[0:E, :]))
            dve.nop().then_inc(group_taken, 1)
            dve.nop().then_inc(logitsT_ready, 1)
            if more:
                l(("k", 0))
                low_item(b, more, "wv'")

            after(("logits", 0))
            link(dve.tensor_copy(logits[:, :, :], bank_of(more, ("logits", 0))
                                 .rearrange("p (i n) -> p i n", n=P)[:, :, 0:E]))
            dve.nop().then_inc(group_taken, 1)
            for i in range(NT):
                link(dve.max(top8[:, i, :], logits[:, i, :]))
                dve.tensor_scalar(negtop[:, i:i + 1], top8[:, i, 0:1], -1.0, None,
                                  ALU.mult).then_inc(negtop_ready, 1)
                link(dve.max_index(arg8[:, i, :], top8[:, i, :], logits[:, i, :]))
                link(dve.tensor_copy(argf[:, i, :], arg8[:, i, :]))
                link(dve.tensor_tensor(
                    hot[:, :, :], iota_e[:, :].unsqueeze(1).to_broadcast([P, K, E]),
                    argf[:, i, 0:K].unsqueeze(2).to_broadcast([P, K, E]), ALU.is_equal))
                link(dve.tensor_reduce(chosen[:, :], hot[:, :, :].rearrange("p k e -> p e k"),
                                       AX.X, ALU.add))
                dve.tensor_copy(chosen_b[:, i, :], chosen[:, :])
                link(dve.tensor_tensor(earlier[:, i + 1, :], earlier[:, i, :], chosen[:, :], ALU.add))
                dve.nop().then_inc(chosen_ready, 1)
                if more and i < 3:
                    l(("k", i + 1))
            for i in range(NT):
                after(("pos", i // 2))
                for k in range(K):
                    last = dve.scalar_tensor_tensor(
                        out=hot[:, k, :], in0=iota_e[:, :], scalar=argf[:, i, k:k + 1],
                        in1=bank_of(more, ("pos", i // 2))[:, (i % 2) * E:(i % 2 + 1) * E],
                        op0=ALU.is_equal, op1=ALU.mult, accum_out=posk[:, i, k:k + 1])
                link(last)
                if i % 2:
                    dve.nop().then_inc(group_taken, 1)
            dve.tensor_scalar(over[:, :, :], posk[:, :, :], float(CAP), OVER, ALU.is_ge, ALU.mult)
            link(dve.scalar_tensor_tensor(out=slotf[:, :, :], in0=posk[:, :, :], scalar=float(E),
                                          in1=argf[:, :, 0:K], op0=ALU.mult, op1=ALU.add))
            link(dve.tensor_tensor(slotf[:, :, :], slotf[:, :, :], over[:, :, :], ALU.add))
            dve.wait_ge(router_exp, (b + 1) * 2 * NT)
            link(dve.reciprocal(einv[:, :], esum[:, :]))
            dve.wait_ge(slots_free, b + 1)
            dve.tensor_copy(slot[:, :, :], slotf[:, :, :])
            dve.tensor_copy(rows[:, :, :, 0], tok[:, :].unsqueeze(2).to_broadcast([P, NT, K]))
            link(dve.tensor_tensor(rows[:, :, :, 1], e8[:, :, 0:K],
                                   einv[:, :].unsqueeze(2).to_broadcast([P, NT, K]), ALU.mult))
            dve.nop().then_inc(rows_ready, 1)
            dve.tensor_copy(earlier[:, 0, :], earlier[:, NT, :])
            link(dve.tensor_scalar(tok[:, :], tok[:, :], float(S), None, ALU.add))
            assert step[0] == (LINKS if more else LINKS - 2), step[0]

        dve.nop().then_inc(group_taken, BANKS)
        dve.nop().then_inc(item_low, 2)
        dve.wait_ge(x_loaded, 16)
        layernorm_stats()
        for name in ("gate", "wq'"):
            low_item(0, "first", name)
        dve.wait_ge(rstd_ready, 1)
        layernorm_apply()
        low_item(0, "first", "wk'")
        for i in range(NT):
            low(0, "first", ("xnT", i))
        low_item(0, "first", "ctxT'")
        for m in range(C):
            low(0, "first", ("q", m))
        low_item(0, "first", "wv'")
        for m in range(C):
            low(0, "first", ("k", m))
        dve.wait_ge(const_ready, 2)
        with dve.Fori(0, B - 1) as b:
            body(b, True)
        body(B - 1, False)

    @block.tensor
    def _(pe):
        def cols(n, width=P):
            return slice(n * width, (n + 1) * width)

        ALL = slice(None)

        def project(b, key, *groups):
            for group in groups:
                kind, m = group
                wt = weight("w" + kind + "'")
                claim(b, key, group)
                if kind == "v":
                    terms = [(at(xnT, ALL, c, cols(m)), at(wt, ALL, c, ALL)) for c in range(C)]
                else:
                    terms = [(at(wt, ALL, c, cols(m)), at(xnT, ALL, c, ALL)) for c in range(C)]
                chain(key, group, terms)

        def at(operand, *index):
            return tuple(h[index] for h in operand)

        def claim(b, key, group):
            pe.wait_ge(group_taken, place(b, key, group) + 1)

        def taken(b, key, group):
            pe.wait_ge(group_taken, place(b, key, group) + 1 + BANKS)

        def item(b, key, name):
            pe.wait_ge(item_low, item_place(b, key, name) + 1 + 2)

        def chain(key, group, terms):
            for n, (still, moving) in enumerate(terms):
                last = product(pe, bank_of(key, group), still, moving, n == 0, n == len(terms) - 1)
            last.then_inc(group_full, 1)

        def transposes(b, key, group, source):
            claim(b, key, group)
            for j in range(4):
                last = pe.transpose(bank_of(key, group)[:, cols(j)], source[:, cols(j)], ident[:, :])
            last.then_inc(group_full, 1)

        def body(b, more):
            def scores_of(i):
                if i >= 2:
                    pe.wait_ge(exp_done, b * NT + i - 1)
                for half_, keys in ((0, ctxT), (1, kT)):
                    for c in range(C):
                        last = product(pe, scores[:, i % 2, cols(half_, S)], at(qT, ALL, c, cols(i)),
                                       at(keys, ALL, c, ALL), c == 0, c == C - 1)
                last.then_inc(scores_full, 1)

            def pT_of(i):
                pe.wait_ge(exp_done, b * NT + i + 1)
                for n in (2 * i, 2 * i + 1):
                    transposes(b, more, ("pT", n), pbuf[:, i % 2, cols(n % 2, 512)])

            def next_xnT(*tiles):
                for i in tiles:
                    pe.wait_ge(xn_ready, (b + 1) * NT + i + 1)
                    transposes(b, more, ("xnT", i), xn[:, i, :])

            pe.wait_ge(item_low, b * len(ITEMS) + len(FIRST_ITEMS) + 2)
            project(b, more, ("v", 0))
            pe.wait_ge(group_taken, b * PER + len(FIRST) + BANKS)
            scores_of(0)
            scores_of(1)
            project(b, more, ("v", 1))
            pT_of(0)
            scores_of(2)
            project(b, more, ("v", 2))
            pT_of(1)
            scores_of(3)
            project(b, more, ("v", 3))
            pT_of(2)
            pT_of(3)
            if more:
                next_xnT(0, 1)
            taken(b, more, ("pT", 2 * NT - 1))
            item(b, more, "ctx")
            for m in range(C):
                claim(b, more, ("av", m))
                chain(more, ("av", m), [(at(cx if c < C else v, ALL, c % C, cols(m)), at(pT, ALL, c, ALL))
                                        for c in range(2 * C)])
            if more:
                next_xnT(2, 3)
            taken(b, more, ("av", C - 1))
            item(b, more, "wo")
            wo = weight("wo")
            for i in range(NT):
                claim(b, more, ("wo", i))
                chain(more, ("wo", i), [(at(qT, ALL, c, cols(i)), at(wo, ALL, c, ALL)) for c in range(C)])
            if more:
                taken(b, more, ("xnT", NT - 1))
                item(b, more, "wq'")
                project(b, more, ("q", 0), ("q", 1))
            for i in range(NT):
                pe.wait_ge(x2_ready, b * NT + i + 1)
                transposes(b, more, ("x2T", i), x2[:, i, :])
            if more:
                project(b, more, ("q", 2), ("q", 3))
            taken(b, more, ("x2T", NT - 1))
            claim(b, more, ("logitsT", 0))
            for c in range(C):
                last = product(pe, bank_of(more, ("logitsT", 0))[0:E, :], at(gate, ALL, c, ALL),
                               at(x2T, ALL, c, ALL), c == 0, c == C - 1)
            last.then_inc(group_full, 1)
            if more:
                item(b, more, "wk'")
                project(b, more, ("k", 0))
            pe.wait_ge(logitsT_ready, b + 1)
            transposes(b, more, ("logits", 0), xn[:, 0, :])
            if more:
                project(b, more, ("k", 1), ("k", 2), ("k", 3))
            for i in range(NT):
                if i % 2 == 0:
                    pe.wait_ge(chosen_ready, b * NT + i + 2)
                    claim(b, more, ("pos", i // 2))
                pos = bank_of(more, ("pos", i // 2))[:, cols(i % 2, E)]
                pe.matmul(pos, before[:, :], chosen_b[:, i, :], start=True, stop=False)
                last = pe.matmul(pos, ones[:, :], earlier[:, i, :], start=False, stop=True)
                if i % 2:
                    last.then_inc(group_full, 1)

        pe.wait_ge(const_ready, 2)
        for i in range(NT):
            pe.wait_ge(xn_ready, i + 1)
            transposes(0, "first", ("xnT", i), xn[:, i, :])
        taken(0, "first", ("xnT", NT - 1))
        item(0, "first", "wq'")
        project(0, "first", *[("q", m) for m in range(C)])
        item(0, "first", "wk'")
        project(0, "first", *[("k", m) for m in range(C)])
        with pe.Fori(0, B - 1) as b:
            body(b, True)
        body(B - 1, False)


def product(pe, out, still, moving, first, last):
    pe.matmul(out, still[0], moving[0], start=first, stop=False)
    pe.matmul(out, still[0], moving[1], start=False, stop=False)
    return pe.matmul(out, still[1], moving[0], start=False, stop=last)


def experts(nc, ctx, t, table, x2_rows):
    def sb(name, shape, dt=F32):
        return ctx.enter_context(nc.sbuf_tensor(name, shape, dt))

    def sem(name):
        return ctx.enter_context(nc.semaphore(name))

    def pair(name, shape):
        return sb(name + "_hi", shape, F32R), sb(name + "_lo", shape, F32R)

    U = 4
    SETS, STEPS = U + 1, U + 2
    ROUNDS = E // U
    assert ROUNDS == T // P
    GU, DN = C * 2 * I, 2 * D
    HP = 2 * P
    gu_raw = sb("gu_raw", [P, 2, GU])
    dn_raw = sb("dn_raw", [P, 2, DN])
    gu = pair("gu", [P, U, GU])
    dn = pair("dn", [P, U, DN])
    sgu = pair("sgu", [P, 2, GU])
    sdn = pair("sdn", [P, 2, DN])
    tab = sb("tab", [P, E, 2])
    own = sb("own", [P, ROUNDS])
    idx_all = sb("idx_all", [P, E + ROUNDS], I32)
    idx = sb("idx", [P, SETS], I32)
    xg = sb("xg", [P, SETS, D])
    xgT = pair("xgT", [P, SETS, D])
    silu = sb("silu", [P, 2, I])
    hid = sb("hid", [P, 2, HP])
    hidT = pair("hidT", [P, 2, HP])
    eo = sb("eo", [P, SETS, D])
    ident = sb("ident_e", [P, P])

    ps_xgT = ctx.enter_context(nc.psum_tensor("ps_xgT", [P, 2, 512], F32))
    ps_gu = ctx.enter_context(nc.psum_tensor("ps_gu", [P, 2, 512], F32))
    ps_hidT = ctx.enter_context(nc.psum_tensor("ps_hidT", [P, 2, 512], F32))
    ps_dn = ctx.enter_context(nc.psum_tensor("ps_dn", [P, 2, 512], F32))

    raw_loaded = [sem("raw_loaded0"), sem("raw_loaded1")]
    gathered = [sem(f"gathered{i}") for i in range(SETS)]
    tab_loaded = sem("tab_loaded")
    own_ready = sem("own_ready")
    idx_ready = sem("idx_ready")
    zero_ready = sem("zero_ready")
    ident_step = sem("ident_step")
    idx_copied = sem("idx_copied")
    weights_high = sem("weights_high")
    weights_split = sem("weights_split")
    xgT_full = sem("xgT_full")
    xgT_high = sem("xgT_high")
    xgT_low = sem("xgT_low")
    gu_full = sem("gu_full")
    silu_ready = sem("silu_ready")
    hid_made = sem("hid_made")
    hidT_full = sem("hidT_full")
    hidT_high = sem("hidT_high")
    hidT_low = sem("hidT_low")
    dn_full = sem("dn_full")
    eo_ready = sem("eo_ready")
    added = sem("added")
    rows_added = sem("rows_added")
    passed = sem("passed_e")

    block = ctx.enter_context(nc.Block())

    def run(eng, step):
        with eng.Fori(0, ROUNDS - 1) as j:
            for q in range(STEPS):
                step(j, q, 2 * STEPS)
        for q in range(STEPS):
            step(ROUNDS - 1, q, STEPS - 1 - q)

    def later(j, q, d):
        return j + (q + d) // STEPS, (q + d) % STEPS

    def rows_of(q):
        return min(q, U)

    def hidden_step(j, q):
        return j * STEPS + q

    def rows_set(j, q):
        return j * SETS + rows_of(q)

    LEAD = 3

    def weights_at(e):
        return e + 2

    def split_target(kind, n):
        if kind == "shared":
            return tuple(h[:, n, :] for h in sgu), tuple(h[:, n, :] for h in sdn)
        return tuple(h[:, n, :] for h in gu), tuple(h[:, n, :] for h in dn)

    FIRST_WEIGHTS = [("expert", 0), ("expert", 1), ("expert", 2), ("shared", 0), ("shared", 1)]

    def splits(split, j, q, behind):
        if q < U and (behind > STEPS or q + LEAD < U):
            u = q + LEAD
            jj, uu = (j, u) if u < U else (j + 1, u - U)
            split(jj, uu)

    @block.sync
    def _(sp):
        def load(kind, e, m_slot, order):
            if order is not None:
                sp.wait_ge(weights_split, order - 1)
            guv, dnv = ((t["gate_up"][e], t["down"][e]) if kind == "expert"
                        else (t["shared_gate_up"][e], t["shared_down"][e]))
            sp.dma_start(gu_raw[:, m_slot, :].rearrange("p (c n) -> p c n", n=2 * I),
                         guv.rearrange("(c p) n -> p c n", p=P)).then_inc(raw_loaded[m_slot], 16)
            sp.dma_start(dn_raw[:, m_slot, 0:D], dnv[0:P, :]).then_inc(raw_loaded[m_slot], 16)
            sp.dma_start(dn_raw[0:I - P, m_slot, D:2 * D], dnv[P:I, :]).then_inc(raw_loaded[m_slot], 16)

        sp.dma_start(tab[:, :, :].rearrange("p e b -> p (e b)"),
                     table.rearrange("(s e) b -> s (e b)", s=CAP)).then_inc(tab_loaded, 16)
        sp.wait_ge(zero_ready, 1)
        for m, (kind, n) in enumerate(FIRST_WEIGHTS):
            load(kind, n, m % 2, m if m >= 2 else None)
        load("expert", LEAD, weights_at(LEAD) % 2, weights_at(LEAD))

        def step(j, q, behind):
            if q < U and behind > STEPS:
                e = j * U + q + U
                load("expert", e, q % 2, weights_at(e))
        run(sp, step)

    @block.gpsimd
    def _(pool):
        pool.iota(own[:, :], [[P, ROUNDS]], base=0, channel_multiplier=1,
                  allow_small_or_imprecise_dtypes=True).then_inc(own_ready, 1)
        pool.memset(ident[:, :], 0.0).then_inc(ident_step, 1)
        pool.wait_ge(ident_step, 1)
        pool.affine_select(out=ident[:, :], in_=ident[:, :], compare_op=ALU.not_equal, fill=1.0,
                           base=0, pattern=[[-1, P]], channel_multiplier=1).then_inc(ident_step, 1)
        pool.nop().then_inc(rows_added, SETS)

        def gather(j, i):
            col = j * U + i if i < U else j + E
            pool.tensor_copy(idx[:, i:i + 1], idx_all[:, bass.ds(col, 1)]).then_inc(idx_copied, 1)
            wait_alone(pool, idx_copied, j * SETS + i + 1, passed)
            pool.indirect_dma_start(
                out=xg[:, i, :], out_offset=None, in_=x2_rows,
                in_offset=bass.IndirectOffsetOnAxis(ap=idx[:, i:i + 1], axis=0)).then_inc(gathered[i], 16)

        pool.wait_ge(idx_ready, 1)
        for i in range(SETS):
            gather(0, i)

        def step(j, q, behind):
            if q == U:
                return
            i = rows_of(q)
            r = j * SETS + i
            wait_alone(pool, eo_ready, r + 1 + 3, passed)
            pool.indirect_dma_start(
                out=t["out"], out_offset=bass.IndirectOffsetOnAxis(ap=idx[:, i:i + 1], axis=0),
                in_=eo[:, i, :], in_offset=None, compute_op=ALU.add).then_inc(added, 16)
            pool.wait_ge(added, (r + 1) * 16)
            pool.sem_inc(rows_added, 1)
            if behind > STEPS:
                gather(j + 1, i)
        run(pool, step)

    @block.scalar
    def _(act):
        def split(kind, n, slot, loads, order):
            to_gu, to_dn = split_target(kind, n)
            act.wait_ge(raw_loaded[slot], loads * 48)
            act.activation(to_gu[0], gu_raw[:, slot, :], ACT.Copy).then_inc(weights_high, 1)
            return lambda: act.activation(to_dn[0], dn_raw[:, slot, :], ACT.Copy).then_inc(weights_high, 1)

        def high_xgT(j, q):
            i = rows_of(q)
            act.wait_ge(xgT_full, j * SETS + i + 1)
            act.activation(xgT[0][:, i, :], ps_xgT[:, i % 2, :], ACT.Copy).then_inc(xgT_high, 1)

        def gate(j, q):
            act.wait_ge(gu_full, hidden_step(j, q) + 1)
            act.activation(silu[:, q % 2, :], ps_gu[:, q % 2, 0:I], ACT.Silu).then_inc(silu_ready, 1)

        act.wait_ge(zero_ready, 1)
        high_xgT(0, 0)
        high_xgT(0, 1)
        for m, (kind, n) in enumerate(FIRST_WEIGHTS):
            split(kind, n, m % 2, m // 2 + 1, m)()
            if m == 0:
                gate(0, 0)

        def step(j, q, behind):
            dn_high = [None]

            def split_of(jj, uu):
                act.wait_ge(dn_full, jj * SETS + uu + 1)
                dn_high[0] = split("expert", uu, uu % 2, jj * (U // 2) + (uu + 2) // 2 + 1, None)

            act.wait_ge(hidT_full, hidden_step(j, q) + 1)
            act.activation(hidT[0][:, q % 2, :], ps_hidT[:, q % 2, 0:HP], ACT.Copy).then_inc(hidT_high, 1)
            if behind >= 2 and later(0, q, 2)[1] != U + 1:
                high_xgT(*later(j, q, 2))
            splits(split_of, j, q, behind)
            if behind >= 1:
                gate(*later(j, q, 1))
            if q != U:
                i = rows_of(q)
                act.wait_ge(dn_full, j * SETS + i + 1 + SETS)
                act.wait_ge(rows_added, j * SETS + i + 1)
                scale = tab[:, bass.ds(j * U + q, 1), 1] if q < U else 1.0
                act.activation(eo[:, i, :], ps_dn[:, i % 2, :], ACT.Copy, scale=scale).then_inc(eo_ready, 1)
            if dn_high[0] is not None:
                dn_high[0]()
        run(act, step)

    @block.vector
    def _(dve):
        dve.memset(hid[:, :, :], 0.0)
        dve.memset(dn_raw[:, :, :], 0.0).then_inc(zero_ready, 1)
        dve.wait_ge(zero_ready, 1)
        dve.nop().then_inc(eo_ready, 3)
        dve.wait_ge(own_ready, 1)
        dve.tensor_copy(idx_all[:, E:E + ROUNDS], own[:, :])
        dve.wait_ge(tab_loaded, 16)
        dve.tensor_copy(idx_all[:, 0:E], tab[:, :, 0]).then_inc(idx_ready, 1)

        def subtract(lo, x, hi):
            return dve.tensor_tensor(lo, x, hi.bitcast(F32), ALU.subtract)

        def split_gu(kind, n, slot, order):
            to_gu, _ = split_target(kind, n)
            dve.wait_ge(weights_high, 2 * order + 1)
            subtract(to_gu[1], gu_raw[:, slot, :], to_gu[0])

        def split_dn(kind, n, slot, order):
            _, to_dn = split_target(kind, n)
            dve.wait_ge(weights_high, 2 * order + 2)
            subtract(to_dn[1], dn_raw[:, slot, :], to_dn[0]).then_inc(weights_split, 1)

        def low_xgT(j, q):
            i = rows_of(q)
            dve.wait_ge(xgT_high, j * SETS + i + 1)
            subtract(xgT[1][:, i, :], ps_xgT[:, i % 2, :], xgT[0][:, i, :]).then_inc(xgT_low, 1)

        def up(j, q):
            dve.wait_ge(silu_ready, hidden_step(j, q) + 1)
            dve.tensor_tensor(hid[:, q % 2, 0:I], silu[:, q % 2, :], ps_gu[:, q % 2, I:2 * I],
                              ALU.mult).then_inc(hid_made, 1)

        low_xgT(0, 0)
        low_xgT(0, 1)
        for m, (kind, n) in enumerate(FIRST_WEIGHTS):
            split_gu(kind, n, m % 2, m)
            split_dn(kind, n, m % 2, m)
            if m == 0:
                up(0, 0)

        def step(j, q, behind):
            dve.wait_ge(hidT_high, hidden_step(j, q) + 1)
            subtract(hidT[1][:, q % 2, :], ps_hidT[:, q % 2, 0:HP], hidT[0][:, q % 2, :]).then_inc(hidT_low, 1)
            if behind >= 2 and later(0, q, 2)[1] != U + 1:
                low_xgT(*later(j, q, 2))
            splits(lambda jj, uu: split_gu("expert", uu, uu % 2, weights_at(jj * U + uu)), j, q, behind)
            if behind >= 1:
                up(*later(j, q, 1))
            splits(lambda jj, uu: split_dn("expert", uu, uu % 2, weights_at(jj * U + uu)), j, q, behind)
        run(dve, step)

    @block.tensor
    def _(pe):
        def cols(n, width=P):
            return slice(n * width, (n + 1) * width)

        def transpose_rows(j, q):
            i = rows_of(q)
            pe.wait_ge(gathered[i], (j + 1) * 16)
            for c in range(C):
                last = pe.transpose(ps_xgT[:, i % 2, cols(c)], xg[:, i, cols(c)], ident[:, :])
            last.then_inc(xgT_full, 1)

        def weights(q):
            kind, n = ("expert", q) if q < U else ("shared", q - U)
            return split_target(kind, n)

        def gate_up(j, q):
            i = rows_of(q)
            pe.wait_ge(xgT_low, j * SETS + i + 1)
            if q >= U:
                pe.wait_ge(weights_split, len(FIRST_WEIGHTS))
            elif isinstance(j, int) and j == 0 and q < LEAD:
                pe.wait_ge(weights_split, q + 1)
            else:
                pe.wait_ge(weights_split, weights_at(j * U + q) + 1)
            w_gu, _ = weights(q)
            for c in range(C):
                last = product(pe, ps_gu[:, q % 2, 0:2 * I], [h[:, i, cols(c)] for h in xgT],
                               [h[:, cols(c, 2 * I)] for h in w_gu], c == 0, c == C - 1)
            last.then_inc(gu_full, 1)

        pe.nop().then_inc(dn_full, SETS)
        pe.wait_ge(ident_step, 2)
        transpose_rows(0, 0)
        transpose_rows(0, 1)
        gate_up(0, 0)

        def step(j, q, behind):
            pe.wait_ge(hid_made, hidden_step(j, q) + 1)
            for c in range(2):
                last = pe.transpose(ps_hidT[:, q % 2, cols(c)], hid[:, q % 2, cols(c)], ident[:, :])
            last.then_inc(hidT_full, 1)
            if behind >= 2 and later(0, q, 2)[1] != U + 1:
                transpose_rows(*later(j, q, 2))
            if behind >= 1:
                gate_up(*later(j, q, 1))
            pe.wait_ge(hidT_low, hidden_step(j, q) + 1)
            i = rows_of(q)
            r = j * SETS + i
            pe.wait_ge(eo_ready, r + (3, 1, 2, 2, 2)[i])
            _, w_dn = weights(q)
            for c in range(2):
                last = product(pe, ps_dn[:, i % 2, :], [h[:, q % 2, cols(c)] for h in hidT],
                               [h[:, cols(c, D)] for h in w_dn], c == 0 and q != U + 1,
                               c == 1 and q != U)
            if q != U:
                last.then_inc(dn_full, 1)
        run(pe, step)


def build(nc, t):
    table = nc.dram_tensor("table", (E * CAP, 2), F32, kind="Internal").ap()
    x2_rows = nc.dram_tensor("x2_rows", (ROWS, D), F32, kind="Internal").ap()
    with ExitStack() as ctx:
        attention_and_router(nc, ctx, t, table, x2_rows)
    with ExitStack() as ctx:
        experts(nc, ctx, t, table, x2_rows)


def kernel(x, ctx_2048, mask_BxSx4224_bf0, L0_xattn_wq, L0_xattn_wk, L0_xattn_wv, L0_xattn_wo,
           L0_ffn_gate_w, L0_ffn_gate_up_proj, L0_ffn_down_proj, L0_ffn_shared_gate_w,
           L0_ffn_shared_up_w, L0_ffn_shared_down_w):
    import concourse.bacc as bacc
    from concourse.bass_utils import run_bass_kernel_spmd

    def chunked(w):
        n = w.shape[1]
        return np.ascontiguousarray(w.reshape(-1, P, n).transpose(1, 0, 2).reshape(P, -1))

    def arr(a):
        return np.asarray(a)

    context = arr(ctx_2048)
    arrays = {
        "x": np.ascontiguousarray(arr(x).reshape(T, D)),
        "ctx": np.ascontiguousarray(context.reshape(T, D)),
        "ctxT": np.stack([chunked(context[b].T) for b in range(B)]),
        "wqT": chunked(arr(L0_xattn_wq).T),
        "wkT": chunked(arr(L0_xattn_wk).T),
        "wvT": chunked(arr(L0_xattn_wv).T),
        "woT": chunked(arr(L0_xattn_wo).T),
        "gateT": chunked(arr(L0_ffn_gate_w).T),
        "shared_gate_up": np.stack([np.concatenate(
            [arr(L0_ffn_shared_gate_w)[h * I:(h + 1) * I].T, arr(L0_ffn_shared_up_w)[h * I:(h + 1) * I].T],
            axis=1) for h in range(2)]),
        "shared_down": np.ascontiguousarray(arr(L0_ffn_shared_down_w).T).reshape(2, I, D),
        "gate_up": np.ascontiguousarray(arr(L0_ffn_gate_up_proj)),
        "down": np.ascontiguousarray(arr(L0_ffn_down_proj)),
    }
    nc = bacc.Bacc("TRN2", target_bir_lowering=False, num_devices=1)
    t = {name: nc.dram_tensor(name + "_in", a.shape, mybir.dt.from_np(a.dtype), kind="ExternalInput").ap()
         for name, a in arrays.items()}
    t["out"] = nc.dram_tensor("out_rows", (ROWS, D), F32, kind="ExternalOutput").ap()
    build(nc, t)
    r = run_bass_kernel_spmd(nc, [{name + "_in": a for name, a in arrays.items()}], core_ids=[0])
    return r.results[0]["out_rows"][0:T].reshape(B, S, D)
```

```python
from contextlib import ExitStack

import numpy as np

import concourse.bass as bass
from concourse import mybir

F32 = mybir.dt.float32
F32R = mybir.dt.float32r
BF16 = mybir.dt.bfloat16
I32 = mybir.dt.int32
U32 = mybir.dt.uint32
ALU = mybir.AluOpType
ACT = mybir.ActivationFunctionType
AX = mybir.AxisListType

P = 128
B, S, D = 4, 512, 512
T = B * S
C = D // P
NT = S // P
KV = 2 * S
E, K, CAP = 64, 6, 128
I = 192
SI = 2 * I
EPS = 1e-5
SCALE = float(D) ** -0.5
ROWS = T + CAP
OVER = float(1 << 20)

BANKS = 4
FIRST = [("xnT", i) for i in range(NT)] + [("q", m) for m in range(C)] + [("k", m) for m in range(C)] + [("v", 0)]


def groups_of(more):
    nxt = more * 1
    return (
        [("pT", n) for n in range(6)] + [("v", 1), ("pT", 6), ("pT", 7), ("v", 2), ("v", 3)]
        + [("av", 0), ("av", 1)] + [("xnT", 0), ("xnT", 1)] * nxt + [("av", 2), ("av", 3)]
        + [("xnT", 2), ("xnT", 3)] * nxt + [("wo", i) for i in range(NT)]
        + [("q", 0), ("q", 1)] * nxt + [("x2T", i) for i in range(NT)] + [("q", 2), ("q", 3)] * nxt
        + [("logitsT", 0)] + [("k", 0)] * nxt + [("logits", 0)]
        + [("k", 1), ("k", 2), ("k", 3), ("v", 0)] * nxt + [("pos", 0), ("pos", 1)]
    )


GROUPS = {"first": FIRST, True: groups_of(True), False: groups_of(False)}
PER = len(GROUPS[True])
assert PER % BANKS == 0
AT = {key: {name: n for n, name in enumerate(groups)} for key, groups in GROUPS.items()}
SPLIT = {key: [g for g in groups if g[0] in ("xnT", "q", "k", "v", "pT", "av", "x2T")]
         for key, groups in GROUPS.items()}
SPLIT_AT = {key: {name: n for n, name in enumerate(groups)} for key, groups in SPLIT.items()}
FIRST_ITEMS = ["gate", "wq'", "wk'", "ctxT'", "wv'"]
ITEMS = ["ctx", "wo", "ctxT'", "wq'", "wk'", "wv'"]
WSLOT = {"wq'": 0, "wk'": 1, "wv'": 0, "wo": 1}


def place(b, key, group):
    return AT[key][group] if key == "first" else len(FIRST) + b * PER + AT[key][group]


def split_place(b, key, group):
    if key == "first":
        return SPLIT_AT[key][group]
    return len(SPLIT["first"]) + b * len(SPLIT[True]) + SPLIT_AT[key][group]


def item_place(b, key, name):
    return FIRST_ITEMS.index(name) if key == "first" else len(FIRST_ITEMS) + b * len(ITEMS) + ITEMS.index(name)


def wait_alone(eng, sem, value, passed):
    eng.wait_ge(sem, value)
    eng.sem_inc(passed, 1)


def attention_and_router(nc, ctx, sem, t, table, x2_rows, kept):
    def sb(name, shape, dt=F32):
        return ctx.enter_context(nc.sbuf_tensor(name, shape, dt))

    def pair(name, shape):
        return sb(name + "_hi", shape, F32R), sb(name + "_lo", shape, F32R)

    ident, slot, rows, own = kept.ident, kept.slot, kept.rows, kept.own
    stage = sb("stage", [P, 2, C * D])
    w = pair("w", [P, 2, C * D])
    gate = pair("gate", [P, C, E])
    xnT = pair("xnT", [P, C, S])
    ctxT = pair("ctxT", [P, C, S])
    cx = pair("cx", [P, C, D])
    qT = pair("qT", [P, C, S])
    kT = pair("kT", [P, C, S])
    v = pair("v", [P, NT, D])
    pT = pair("pT", [P, KV // P, S])
    x2T = tuple(h[:, 0:C, :] for h in pT)
    pbuf = sb("pbuf", [P, 2, KV])
    x2 = pbuf[:, :, :].rearrange("p a (b d) -> p (a b) d", d=D)
    xn = sb("xn", [P, NT, D])
    logitsT = xn[0:E, 0, :]
    hot = xn[:, 1:, :].rearrange("p a (b e) -> p (a b) e", e=E)
    assert (NT - 1) * D == NT * K * E
    chosen = xn[:, 0, 0:NT * E].rearrange("p (i e) -> p i e", e=E)
    res = sb("res", [P, NT, D])
    before = sb("before", [P, P], BF16)
    ones = sb("ones", [P, P], BF16)
    iota_e = sb("iota_e", [P, E])
    half = sb("half", [P, NT])
    stats = sb("stats", [P, NT, 6])
    mv = sb("mv", [P, NT, 2])
    veps = sb("veps", [P, NT])
    rstd = sb("rstd", [P, NT])
    stats2 = sb("stats2", [P, NT, 6])
    mv2 = sb("mv2", [P, NT, 2])
    veps2 = sb("veps2", [P, NT])
    rstd2 = sb("rstd2", [P, NT])
    mx = sb("mx", [P, NT])
    negmax = sb("negmax", [P, NT])
    rowsum = sb("rowsum", [P, NT])
    rinv = sb("rinv", [P, NT])
    logits = sb("logits", [P, NT, E])
    top8 = sb("top8", [P, NT, 8])
    arg8 = sb("arg8", [P, NT, 8], U32)
    argf = sb("argf", [P, NT, K])
    negtop = sb("negtop", [P, NT])
    e8 = sb("e8", [P, NT, 8])
    elogits = sb("elogits", [P, E])
    esum = sb("esum", [P, NT])
    einv = sb("einv", [P, NT])
    chosen_b = sb("chosen_b", [P, NT, E], BF16)
    earlier = sb("earlier", [P, NT + 1, E], BF16)
    posk = sb("posk", [P, NT, K])
    over = sb("over", [P, NT, K])
    slotf = sb("slotf", [P, NT, K])
    tok = sb("tok", [P, NT])

    bank = ctx.enter_context(nc.psum_tensor("bank", [P, BANKS, 512], F32))
    scores = ctx.enter_context(nc.psum_tensor("scores", [P, 2, KV], F32))

    stage_loaded = [sem("stage_loaded0"), sem("stage_loaded1")]
    item_high = sem("item_high")
    item_low = sem("item_low")
    x_loaded = sem("x_loaded")
    x_tile_loaded = [sem(f"x_tile_loaded{i}") for i in range(NT)]
    res_loaded = sem("res_loaded")
    group_full = sem("group_full")
    group_taken = sem("group_taken")
    high_done = sem("high_done")
    vec_step = sem("vec_step")
    xn_ready = sem("xn_ready")
    scores_full = sem("scores_full")
    negmax_ready = sem("negmax_ready")
    exp_done = sem("exp_done")
    var_ready = sem("var_ready")
    rstd_ready = sem("rstd_ready")
    x2_ready = sem("x2_ready")
    x2_stored = sem("x2_stored")
    logitsT_ready = sem("logitsT_ready")
    negtop_ready = sem("negtop_ready")
    router_exp = sem("router_exp")
    chosen_ready = sem("chosen_ready")
    rows_ready = sem("rows_ready")
    scattered = sem("scattered")
    slots_free = sem("slots_free")
    base_ready = sem("base_ready")
    base_stored = sem("base_stored")
    const_ready = sem("const_ready")
    pool_step = sem("pool_step")
    pads_stored = sem("pads_stored")
    passed = sem("passed")
    kept.rows_ready, kept.slots_free = rows_ready, slots_free
    kept.group_full, kept.projected = group_full, place(B - 1, False, ("wo", NT - 1)) + 1

    x_v = t["x"].rearrange("(b i p) d -> b p i d", b=B, p=P)
    out_v = t["out"][0:T, :].rearrange("(b i p) d -> b i p d", b=B, p=P)
    x2_v = x2_rows[0:T, :].rearrange("(b i p) d -> b i p d", b=B, p=P)
    ctx_v = t["ctx"].rearrange("(b i p) d -> b p i d", b=B, p=P)
    weight_source = {"wq'": t["wqT"], "wk'": t["wkT"], "wv'": t["wvT"], "wo": t["woT"]}

    def flat(operand):
        return tuple(h[:, :, :].rearrange("p c n -> p (c n)") for h in operand)

    def weight(name):
        return tuple(h[:, WSLOT[name], :].rearrange("p (c n) -> p c n", n=D) for h in w)

    def item_dest(name):
        if name in WSLOT:
            return tuple(h[:, WSLOT[name], :] for h in w)
        return flat({"ctxT'": ctxT, "ctx": cx, "gate": gate}[name])

    def item_stage(b, key, name):
        parity = (FIRST_ITEMS.index(name) if key == "first"
                  else len(FIRST_ITEMS) + ITEMS.index(name)) % 2
        return stage[:, parity, 0:(C * E if name == "gate" else C * D)]

    def split_dest(group):
        kind, n = group
        if kind in ("xnT", "x2T"):
            return tuple(h[:, :, n * P:(n + 1) * P] for h in (xnT if kind == "xnT" else x2T))
        if kind == "pT":
            i, c = n // 2, (n % 2) * 4
            return tuple(h[:, c:c + 4, i * P:(i + 1) * P] for h in pT)
        to = {"q": qT, "k": kT, "v": v, "av": qT}[kind]
        return tuple(h[:, n:n + 1, :] for h in to)

    def bank_of(key, group):
        return bank[:, (AT[key][group] + (0 if key == "first" else len(FIRST))) % BANKS, :]

    def split_source(key, group):
        inner = P if group[0] in ("xnT", "x2T", "pT") else 512
        return bank_of(key, group).rearrange("p (c n) -> p c n", n=inner)

    def sync(sp):
        def load_item(b, key, name, source_batch=None):
            n = item_place(b, key, name)
            sp.wait_ge(item_low, n + 1)
            dst = item_stage(b, key, name)
            if name == "gate":
                src = t["gateT"]
            elif name == "ctxT'":
                src = t["ctxT"][source_batch]
            elif name == "ctx":
                dst = dst.rearrange("p (c n) -> p c n", n=D)
                src = ctx_v[source_batch]
            else:
                src = weight_source[name]
            parity = (FIRST_ITEMS.index(name) if key == "first"
                      else len(FIRST_ITEMS) + ITEMS.index(name)) % 2
            sp.dma_start(dst, src).then_inc(stage_loaded[parity], 16)

        def body(b, more):
            load_item(b, more, "ctx", b)
            load_item(b, more, "wo")
            if more:
                sp.wait_ge(group_taken, b * PER + len(FIRST) + BANKS)
                sp.dma_start(xn[:, :, :], x_v[b + 1]).then_inc(x_loaded, 16)
            sp.wait_ge(base_stored, b * 16 * NT + 16 * NT)
            sp.dma_start(res[:, :, :], x_v[b]).then_inc(res_loaded, 16)
            if more:
                for name in ("ctxT'", "wq'", "wk'"):
                    load_item(b, more, name, b + 1)
            for i in range(NT):
                sp.wait_ge(base_ready, b * NT + i + 1)
                sp.dma_start(out_v[b, i], res[:, i, :]).then_inc(base_stored, 16)
                sp.wait_ge(x2_ready, b * NT + i + 1)
                sp.dma_start(x2_v[b, i], x2[:, i, :]).then_inc(x2_stored, 16)
            if more:
                load_item(b, more, "wv'")

        sp.nop().then_inc(base_stored, 16 * NT)
        for i in range(NT):
            sp.dma_start(xn[:, i, :], x_v[0][:, i, :]).then_inc(x_tile_loaded[i], 16)
        sp.wait_ge(const_ready, 1)
        for name in FIRST_ITEMS:
            load_item(0, "first", name, 0)
        pad_rows = pbuf[:, 0, 0:2 * E]
        zero_rows = pbuf[:, 1, 0:D]
        sp.dma_start(table.rearrange("(s e) b -> s (e b)", s=CAP), pad_rows).then_inc(pads_stored, 16)
        sp.dma_start(x2_rows[T:ROWS, :], zero_rows).then_inc(pads_stored, 16)
        sp.dma_start(t["out"][T:ROWS, :], zero_rows).then_inc(pads_stored, 16)
        with sp.Fori(0, B - 1) as b:
            body(b, True)
        body(B - 1, False)
        sp.wait_ge(base_stored, 16 * NT * (B + 1))
        sp.wait_ge(x2_stored, 16 * NT * B)
        sp.wait_ge(pads_stored, 48)

    def gpsimd(pool):
        steps = [0]

        def link(ins):
            steps[0] += 1
            ins.then_inc(pool_step, 1)
            pool.wait_ge(pool_step, steps[0])

        pool.memset(pbuf[:, 0, 0:2 * E], 0.0)
        pool.memset(pbuf[:, 1, 0:D], 0.0)
        pool.iota(own[:, :], [[P, T // P]], base=0, channel_multiplier=1,
                  allow_small_or_imprecise_dtypes=True)
        link(pool.memset(ident[:, :], 0.0))
        pads = pbuf[:, 0, 0:2 * E].rearrange("p (e b) -> p e b", b=2)
        link(pool.iota(pads[:, :, 0], [[0, E]], base=T, channel_multiplier=1,
                       allow_small_or_imprecise_dtypes=True))
        pool.nop().then_inc(const_ready, 1)
        pool.affine_select(out=ident[:, :], in_=ident[:, :], compare_op=ALU.not_equal, fill=1.0,
                           base=0, pattern=[[-1, P]], channel_multiplier=1)
        pool.memset(half[:, :], -0.5)
        pool.memset(ones[:, :], 1.0)
        link(pool.memset(before[:, :], 1.0))
        pool.affine_select(out=before[:, :], in_=before[:, :], compare_op=ALU.is_ge, fill=0.0,
                           base=-1, pattern=[[1, P]], channel_multiplier=-1)
        pool.iota(iota_e[:, :], [[1, E]], base=0, channel_multiplier=0,
                  allow_small_or_imprecise_dtypes=True)
        pool.iota(tok[:, :], [[P, NT]], base=0, channel_multiplier=1,
                  allow_small_or_imprecise_dtypes=True)
        link(pool.memset(earlier[:, 0, :], 0.0))
        pool.nop().then_inc(const_ready, 1)
        pool.nop().then_inc(slots_free, 1)

        def first_norm(n):
            pool.wait_ge(var_ready, n + 1)
            pool.tensor_tensor(rstd[:, :], veps[:, :], half[:, :], ALU.pow).then_inc(rstd_ready, 1)

        def body(b, more):
            for i in range(NT):
                pool.wait_ge(var_ready, b * (NT + 1) + 1 + (1 if more else 0) + i + 1)
                pool.tensor_tensor(rstd2[:, i:i + 1], veps2[:, i:i + 1], half[:, 0:1],
                                   ALU.pow).then_inc(rstd_ready, 1)
            for i in range(NT):
                if i % 2 == 0:
                    wait_alone(pool, rows_ready, 2 * b + i // 2 + 1, passed)
                if i == 3 and not isinstance(b, int):
                    first_norm((b + 1) * (NT + 1) + 1)
                for k in range(K):
                    pool.indirect_dma_start(
                        out=table, out_offset=bass.IndirectOffsetOnAxis(ap=slot[:, i, k:k + 1], axis=0),
                        in_=rows[:, i, k, :], in_offset=None, bounds_check=E * CAP - 1,
                        oob_is_err=False).then_inc(scattered, 16)
            pool.wait_ge(scattered, (b + 1) * 16 * NT * K)
            pool.sem_inc(slots_free, 1)

        first_norm(0)
        pool.wait_ge(pads_stored, 48)
        first_norm(1)
        with pool.Fori(0, B - 2) as b:
            body(b, True)
        body(B - 2, True)
        body(B - 1, False)

    def scalar(act):
        def high_item(b, key, name):
            n = (FIRST_ITEMS.index(name) if key == "first" else len(FIRST_ITEMS) + ITEMS.index(name))
            loads = n // 2 + 1 if key == "first" else b * (len(ITEMS) // 2) + n // 2 + 1
            act.wait_ge(stage_loaded[n % 2], loads * 16)
            act.activation(item_dest(name)[0], item_stage(b, key, name), ACT.Copy).then_inc(item_high, 1)

        def after(b, key, group):
            act.wait_ge(group_full, place(b, key, group) + 1)

        def high(b, key, group):
            after(b, key, group)
            act.activation(split_dest(group)[0], split_source(key, group), ACT.Copy).then_inc(high_done, 1)

        def exp(b, i):
            act.wait_ge(negmax_ready, b * NT + i + 1)
            act.activation(pbuf[:, i % 2, :], scores[:, i % 2, :], ACT.Exp,
                           bias=negmax[:, i:i + 1], scale=SCALE,
                           accum_out=rowsum[:, i:i + 1]).then_inc(exp_done, 1)

        def body(b, more):
            def h(*groups):
                for group in groups:
                    high(b, more, group)

            h(("pT", 0), ("pT", 1))
            exp(b, 2)
            high_item(b, more, "ctx")
            h(("pT", 2), ("pT", 3))
            exp(b, 3)
            h(("pT", 4), ("pT", 5), ("v", 1), ("pT", 6), ("pT", 7), ("v", 2), ("v", 3))
            high_item(b, more, "wo")
            h(("av", 0), ("av", 1))
            if more:
                h(("xnT", 0), ("xnT", 1))
                high_item(b, more, "ctxT'")
            h(("av", 2), ("av", 3))
            if more:
                h(("xnT", 2), ("xnT", 3))
                high_item(b, more, "wq'")
            if more:
                h(("q", 0), ("q", 1))
            h(*[("x2T", i) for i in range(NT)])
            if more:
                high_item(b, more, "wk'")
                h(("q", 2), ("q", 3))
                high_item(b, more, "wv'")
                h(("k", 0))
            act.wait_ge(negtop_ready, b + 1)
            for i in range(NT):
                if i:
                    act.wait_ge(router_exp, (b * NT + i) * 2)
                act.activation(elogits[:, :], logits[:, i, :], ACT.Exp, bias=negtop[:, i:i + 1],
                               accum_out=esum[:, i:i + 1]).then_inc(router_exp, 1)
                act.activation(e8[:, i, :], top8[:, i, :], ACT.Exp,
                               bias=negtop[:, i:i + 1]).then_inc(router_exp, 1)
                if more and i == 1:
                    h(("k", 1))
            if more:
                h(("k", 2), ("k", 3))
            if more:
                h(("v", 0))
                act.wait_ge(x2_stored, (b + 1) * 16 * NT)
                exp(b + 1, 0)
                exp(b + 1, 1)

        for name in ("gate", "wq'"):
            high_item(0, "first", name)
        for i in range(NT):
            high(0, "first", ("xnT", i))
        for name in ("wk'", "ctxT'"):
            high_item(0, "first", name)
        for m in range(C):
            high(0, "first", ("q", m))
        high_item(0, "first", "wv'")
        for m in range(C):
            high(0, "first", ("k", m))
        high(0, "first", ("v", 0))
        act.wait_ge(pads_stored, 48)
        exp(0, 0)
        exp(0, 1)
        with act.Fori(0, B - 1) as b:
            body(b, True)
        body(B - 1, False)

    def vector(dve):
        LINKS = 38
        first = [0]
        step = [0]
        batch = [None]

        def link(ins, alone=False):
            step[0] += 1
            ins.then_inc(vec_step, 1)
            if batch[0] is None:
                first[0] = step[0]
                dve.wait_ge(vec_step, step[0])
            elif alone:
                wait_alone(dve, vec_step, batch[0] * LINKS + first[0] + step[0], passed)
            else:
                dve.wait_ge(vec_step, batch[0] * LINKS + first[0] + step[0])

        def low_item(b, key, name):
            dve.wait_ge(item_high, item_place(b, key, name) + 1)
            hi, lo = item_dest(name)
            dve.tensor_tensor(lo, item_stage(b, key, name), hi.bitcast(F32),
                              ALU.subtract).then_inc(item_low, 1)

        def low(b, key, group):
            dve.wait_ge(high_done, split_place(b, key, group) + 1)
            hi, lo = split_dest(group)
            dve.tensor_tensor(lo, split_source(key, group), hi.bitcast(F32),
                              ALU.subtract).then_inc(group_taken, 1)

        def layernorm_stats(by_tile=False):
            for i in range(NT):
                if by_tile:
                    dve.wait_ge(x_tile_loaded[i], 16)
                last = dve.bn_stats(stats[:, i, :], xn[:, i, :])
            link(last, alone=True)
            for i in range(NT):
                last = dve.bn_aggr(mv[:, i, :], stats[:, i, :])
            link(last)
            dve.tensor_scalar(veps[:, :], mv[:, :, 1], EPS, None, ALU.add).then_inc(var_ready, 1)

        def layernorm_apply():
            for i in range(NT):
                dve.tensor_scalar(xn[:, i, :], xn[:, i, :], mv[:, i, 0:1], rstd[:, i:i + 1],
                                  ALU.subtract, ALU.mult).then_inc(xn_ready, 1)

        def maximum(b, i):
            dve.wait_ge(scores_full, b * NT + i + 1)
            link(dve.reduce_max(mx[:, i:i + 1], scores[:, i % 2, :], AX.X))
            dve.tensor_scalar(negmax[:, i:i + 1], mx[:, i:i + 1], -SCALE, None,
                              ALU.mult).then_inc(negmax_ready, 1)

        def body(b, more):
            step[0] = 0
            batch[0] = b

            def after(group):
                dve.wait_ge(group_full, place(b, more, group) + 1)

            def l(*groups):
                for group in groups:
                    low(b, more, group)

            def second_norm(i):
                dve.wait_ge(rstd_ready, b * (NT + 1) + 1 + (1 if more else 0) + i + 1)
                dve.tensor_scalar(x2[:, i, :], res[:, i, :], mv2[:, i, 0:1], rstd2[:, i:i + 1],
                                  ALU.subtract, ALU.mult).then_inc(x2_ready, 1)

            maximum(b, 2)
            l(*[("pT", n) for n in range(4)])
            maximum(b, 3)
            low_item(b, more, "ctx")
            l(("pT", 4), ("pT", 5), ("v", 1), ("pT", 6), ("pT", 7), ("v", 2), ("v", 3))
            if more:
                dve.wait_ge(x_loaded, (b + 1) * 16)
                layernorm_stats()
            low_item(b, more, "wo")
            l(("av", 0))
            if more:
                dve.wait_ge(rstd_ready, b * (NT + 1) + 2)
                layernorm_apply()
            l(("av", 1))
            if more:
                l(("xnT", 0), ("xnT", 1))
                low_item(b, more, "ctxT'")
            l(("av", 2), ("av", 3))
            if more:
                l(("xnT", 2), ("xnT", 3))
                low_item(b, more, "wq'")
            dve.wait_ge(exp_done, b * NT + NT)
            link(dve.reciprocal(rinv[:, :], rowsum[:, :]))
            dve.wait_ge(res_loaded, (b + 1) * 16)

            for i in range(NT):
                after(("wo", i))
                link(dve.scalar_tensor_tensor(out=res[:, i, :], in0=bank_of(more, ("wo", i)),
                                              scalar=rinv[:, i:i + 1], in1=res[:, i, :],
                                              op0=ALU.mult, op1=ALU.add))
                dve.nop().then_inc(group_taken, 1)
                dve.nop().then_inc(base_ready, 1)
                link(dve.bn_stats(stats2[:, i, :], res[:, i, :]), alone=True)
                link(dve.bn_aggr(mv2[:, i, :], stats2[:, i, :]))
                dve.tensor_scalar(veps2[:, i:i + 1], mv2[:, i, 1:2], EPS, None,
                                  ALU.add).then_inc(var_ready, 1)
                if i:
                    second_norm(i - 1)
            if not more:
                l(("x2T", 0))
            second_norm(NT - 1)
            if more:
                l(("q", 0), ("q", 1), ("x2T", 0))
            l(*[("x2T", i) for i in range(1, NT)])
            if more:
                low_item(b, more, "wk'")
                l(("q", 2), ("q", 3))
            after(("logitsT", 0))
            link(dve.tensor_copy(logitsT, bank_of(more, ("logitsT", 0))[0:E, :]))
            dve.nop().then_inc(group_taken, 1)
            dve.nop().then_inc(logitsT_ready, 1)
            if more:
                l(("k", 0))
                low_item(b, more, "wv'")

            after(("logits", 0))
            link(dve.tensor_copy(logits[:, :, :], bank_of(more, ("logits", 0))
                                 .rearrange("p (i n) -> p i n", n=P)[:, :, 0:E]))
            dve.nop().then_inc(group_taken, 1)
            for i in range(NT):
                last = dve.max(top8[:, i, :], logits[:, i, :])
            link(last)
            dve.tensor_scalar(negtop[:, :], top8[:, :, 0], -1.0, None, ALU.mult).then_inc(negtop_ready, 1)
            for i in range(NT):
                last = dve.max_index(arg8[:, i, :], top8[:, i, :], logits[:, i, :])
            link(last)
            link(dve.tensor_copy(argf[:, :, :], arg8[:, :, 0:K]))
            if more:
                l(("k", 1))
            link(dve.tensor_tensor(
                hot, iota_e[:, :].unsqueeze(1).to_broadcast([P, NT * K, E]),
                argf[:, :, :].rearrange("p i k -> p (i k)").unsqueeze(2).to_broadcast([P, NT * K, E]),
                ALU.is_equal))
            if more:
                l(("k", 2), ("k", 3))
            for i in range(NT):
                last = dve.tensor_reduce(chosen[:, i, :], hot[:, i * K:(i + 1) * K, :]
                                         .rearrange("p k e -> p e k"), AX.X, ALU.add)
            link(last)
            dve.tensor_copy(chosen_b[:, :, :], chosen[:, :, :])
            for i in range(NT):
                link(dve.tensor_tensor(earlier[:, i + 1, :], earlier[:, i, :], chosen[:, i, :], ALU.add))
            dve.nop().then_inc(chosen_ready, 1)
            if more:
                l(("v", 0))
                maximum(b + 1, 0)
            dve.wait_ge(router_exp, (b + 1) * 2 * NT)
            link(dve.reciprocal(einv[:, :], esum[:, :]))
            dve.wait_ge(slots_free, b + 1)
            for n in range(2):
                two = slice(2 * n, 2 * n + 2)
                after(("pos", n))
                for i in (2 * n, 2 * n + 1):
                    for k in range(K):
                        last = dve.scalar_tensor_tensor(
                            out=hot[:, i * K + k, :], in0=iota_e[:, :], scalar=argf[:, i, k:k + 1],
                            in1=bank_of(more, ("pos", n))[:, (i % 2) * E:(i % 2 + 1) * E],
                            op0=ALU.is_equal, op1=ALU.mult, accum_out=posk[:, i, k:k + 1])
                link(last)
                dve.nop().then_inc(group_taken, 1)
                dve.tensor_scalar(over[:, two, :], posk[:, two, :], float(CAP), OVER, ALU.is_ge, ALU.mult)
                link(dve.scalar_tensor_tensor(out=slotf[:, two, :], in0=posk[:, two, :], scalar=float(E),
                                              in1=argf[:, two, :], op0=ALU.mult, op1=ALU.add))
                dve.tensor_copy(rows[:, two, :, 0], tok[:, two].unsqueeze(2).to_broadcast([P, 2, K]))
                dve.tensor_tensor(rows[:, two, :, 1], e8[:, two, 0:K],
                                  einv[:, two].unsqueeze(2).to_broadcast([P, 2, K]), ALU.mult)
                link(dve.tensor_tensor(slot[:, two, :], slotf[:, two, :], over[:, two, :], ALU.add))
                dve.nop().then_inc(rows_ready, 1)
            if more:
                dve.tensor_copy(earlier[:, 0, :], earlier[:, NT, :])
                link(dve.tensor_scalar(tok[:, :], tok[:, :], float(S), None, ALU.add))
            if more:
                maximum(b + 1, 1)
            assert step[0] == (LINKS if more else LINKS - 5), step[0]

        dve.nop().then_inc(group_taken, BANKS)
        dve.nop().then_inc(item_low, 2)
        layernorm_stats(by_tile=True)
        low_item(0, "first", "gate")
        dve.wait_ge(rstd_ready, 1)
        layernorm_apply()
        low_item(0, "first", "wq'")
        for i in range(NT):
            low(0, "first", ("xnT", i))
        low_item(0, "first", "wk'")
        low_item(0, "first", "ctxT'")
        for m in range(C):
            low(0, "first", ("q", m))
        low_item(0, "first", "wv'")
        for m in range(C):
            low(0, "first", ("k", m))
        low(0, "first", ("v", 0))
        maximum(0, 0)
        maximum(0, 1)
        dve.wait_ge(const_ready, 2)
        with dve.Fori(0, B - 1) as b:
            body(b, True)
        body(B - 1, False)

    def tensor(pe):
        def cols(n, width=P):
            return slice(n * width, (n + 1) * width)

        ALL = slice(None)

        def project(b, key, *groups):
            for group in groups:
                kind, m = group
                wt = weight("w" + kind + "'")
                claim(b, key, group)
                if kind == "v":
                    terms = [(at(xnT, ALL, c, cols(m)), at(wt, ALL, c, ALL)) for c in range(C)]
                else:
                    terms = [(at(wt, ALL, c, cols(m)), at(xnT, ALL, c, ALL)) for c in range(C)]
                chain(key, group, terms)

        def at(operand, *index):
            return tuple(h[index] for h in operand)

        def claim(b, key, group):
            pe.wait_ge(group_taken, place(b, key, group) + 1)

        def taken(b, key, group):
            pe.wait_ge(group_taken, place(b, key, group) + 1 + BANKS)

        def item(b, key, name):
            pe.wait_ge(item_low, item_place(b, key, name) + 1 + 2)

        def chain(key, group, terms):
            for n, (still, moving) in enumerate(terms):
                last = product(pe, bank_of(key, group), still, moving, n == 0, n == len(terms) - 1)
            last.then_inc(group_full, 1)

        def transposes(b, key, group, source):
            claim(b, key, group)
            for j in range(4):
                last = pe.transpose(bank_of(key, group)[:, cols(j)], source[:, cols(j)], ident[:, :])
            last.then_inc(group_full, 1)

        def scores_of(b, i):
            if i >= 2:
                pe.wait_ge(exp_done, b * NT + i - 1)
            for half_, keys in ((0, ctxT), (1, kT)):
                for c in range(C):
                    last = product(pe, scores[:, i % 2, cols(half_, S)], at(qT, ALL, c, cols(i)),
                                   at(keys, ALL, c, ALL), c == 0, c == C - 1)
            last.then_inc(scores_full, 1)

        def body(b, more):
            def pT_of(i):
                pe.wait_ge(exp_done, b * NT + i + 1)
                for n in (2 * i, 2 * i + 1):
                    transposes(b, more, ("pT", n), pbuf[:, i % 2, cols(n % 2, 512)])

            def next_xnT(*tiles):
                for i in tiles:
                    pe.wait_ge(xn_ready, (b + 1) * NT + i + 1)
                    transposes(b, more, ("xnT", i), xn[:, i, :])

            pT_of(0)
            scores_of(b, 2)
            pT_of(1)
            scores_of(b, 3)
            pT_of(2)
            project(b, more, ("v", 1))
            pT_of(3)
            project(b, more, ("v", 2), ("v", 3))
            item(b, more, "ctx")
            taken(b, more, ("pT", 2 * NT - 1))
            for m in range(C):
                claim(b, more, ("av", m))
                for c in range(2 * C):
                    if m == 0 and c == C:
                        taken(b, more, ("v", C - 1))
                    last = product(pe, bank_of(more, ("av", m)), at(cx if c < C else v, ALL, c % C, cols(m)),
                                   at(pT, ALL, c, ALL), c == 0, c == 2 * C - 1)
                last.then_inc(group_full, 1)
                if more and m == 1:
                    next_xnT(0, 1)
            if more:
                next_xnT(2, 3)
            taken(b, more, ("av", C - 1))
            item(b, more, "wo")
            wo = weight("wo")
            for i in range(NT):
                claim(b, more, ("wo", i))
                chain(more, ("wo", i), [(at(qT, ALL, c, cols(i)), at(wo, ALL, c, ALL)) for c in range(C)])
            if more:
                taken(b, more, ("xnT", NT - 1))
                item(b, more, "wq'")
                project(b, more, ("q", 0), ("q", 1))
            for i in range(NT):
                pe.wait_ge(x2_ready, b * NT + i + 1)
                transposes(b, more, ("x2T", i), x2[:, i, :])
            if more:
                project(b, more, ("q", 2), ("q", 3))
            taken(b, more, ("x2T", NT - 1))
            claim(b, more, ("logitsT", 0))
            for c in range(C):
                last = product(pe, bank_of(more, ("logitsT", 0))[0:E, :], at(gate, ALL, c, ALL),
                               at(x2T, ALL, c, ALL), c == 0, c == C - 1)
            last.then_inc(group_full, 1)
            if more:
                item(b, more, "wk'")
                project(b, more, ("k", 0))
            pe.wait_ge(logitsT_ready, b + 1)
            transposes(b, more, ("logits", 0), xn[:, 0, :])
            if more:
                project(b, more, ("k", 1), ("k", 2), ("k", 3))
                item(b, more, "wv'")
                project(b, more, ("v", 0))
                taken(b, more, ("k", 3))
                scores_of(b + 1, 0)
            for i in range(NT):
                if i % 2 == 0:
                    pe.wait_ge(chosen_ready, b + 1)
                    claim(b, more, ("pos", i // 2))
                pos = bank_of(more, ("pos", i // 2))[:, cols(i % 2, E)]
                pe.matmul(pos, before[:, :], chosen_b[:, i, :], start=True, stop=False)
                last = pe.matmul(pos, ones[:, :], earlier[:, i, :], start=False, stop=True)
                if i % 2:
                    last.then_inc(group_full, 1)
            if more:
                scores_of(b + 1, 1)

        pe.wait_ge(const_ready, 2)
        for i in range(NT):
            pe.wait_ge(xn_ready, i + 1)
            transposes(0, "first", ("xnT", i), xn[:, i, :])
        taken(0, "first", ("xnT", NT - 1))
        item(0, "first", "wq'")
        project(0, "first", *[("q", m) for m in range(C)])
        item(0, "first", "wk'")
        project(0, "first", *[("k", m) for m in range(C)])
        item(0, "first", "wv'")
        project(0, "first", ("v", 0))
        taken(0, "first", ("k", C - 1))
        scores_of(0, 0)
        scores_of(0, 1)
        with pe.Fori(0, B - 1) as b:
            body(b, True)
        body(B - 1, False)

    return Programs(sync, gpsimd, scalar, vector, tensor)


def product(pe, out, still, moving, first, last):
    pe.matmul(out, still[0], moving[0], start=first, stop=False)
    pe.matmul(out, still[0], moving[1], start=False, stop=False)
    return pe.matmul(out, still[1], moving[0], start=False, stop=last)


def experts(nc, ctx, sem, t, table, x2_rows, kept):
    def sb(name, shape, dt=F32):
        return ctx.enter_context(nc.sbuf_tensor(name, shape, dt))

    def pair(name, shape):
        return sb(name + "_hi", shape, F32R), sb(name + "_lo", shape, F32R)

    U, G, WARM = 16, 3, 4
    ROUNDS = E // U
    assert WARM + ROUNDS * G == T // P
    STEP = []
    for i in range(U + G):
        tiles = i * G // (U + G)
        if (i + 1) * G // (U + G) > tiles:
            STEP += [("shared", tiles, half, i) for half in range(2)]
        else:
            STEP += [("expert", i - tiles, None, i)]
    STEPS, SETS = len(STEP), U + G
    step_of_expert = {n: q for q, (kind, n, _, _) in enumerate(STEP) if kind == "expert"}
    RING = 4
    XG = 5
    AHEAD = 7
    GU = C * 2 * I
    HP = 2 * P
    RAW = 4
    PIECES = 3
    XGT = [i % 2 for i in range(SETS - 1)] + [2]
    gu_raw = sb("gu_raw", [P, RAW, GU])
    dn_raw = sb("dn_raw", [P, RAW, 2 * D])
    xg = sb("xg", [P, XG, D])
    assert RAW * (GU + 2 * D) + WARM * D <= 6 * C * D and WARM < XG
    sgu = pair("sgu", [P, 2, GU])
    sdn = sb("sdn_hi", [P, 2, 2 * D], F32R), sb("sdn_lo", [P, 2, D], F32R)
    xgT = pair("xgT", [P, 3, D])
    assert RAW * (GU + 2 * D) + XG * D + 4 * GU + 6 * D + 6 * D <= 12 * C * D + 2 * C * E
    gu = pair("gu", [P, RING, GU])
    dn = sb("dn_hi", [P, RING, 2 * D], F32R), sb("dn_lo", [P, RING, D], F32R)
    tab = sb("tab", [P, E, 2])
    idx_all = sb("idx_all", [P, E + T // P], I32)
    idx_in = sb("idx_in", [P, XG], I32)
    idx_out = sb("idx_out", [P, XG], I32)
    silu = sb("silu", [P, 2, I])
    hid = sb("hid", [P, 2, HP])
    hidT = pair("hidT", [P, 2, HP])
    eo = sb("eo", [P, XG, D])
    ident, own = kept.ident, kept.own

    ps_hidT = ctx.enter_context(nc.psum_tensor("ps_hidT", [P, 2, 512], F32))
    ps_dn = ctx.enter_context(nc.psum_tensor("ps_dn", [P, 2, 512], F32))
    ps_gu = ctx.enter_context(nc.psum_tensor("ps_gu", [P, 2, 512], F32))
    ps_xgT = ctx.enter_context(nc.psum_tensor("ps_xgT", [P, 2, 512], F32))

    raw_loaded = [[sem(f"raw_loaded{i}_{part}") for part in range(PIECES)] for i in range(RAW)]
    gathered = [sem(f"gathered{i}") for i in range(XG)]
    tab_loaded = sem("tab_loaded")
    idx_ready = sem("idx_ready")
    warm_loaded = [sem(f"warm_loaded{m}") for m in range(WARM)]
    warm_base_loaded = sem("warm_base_loaded")
    warm_stored = sem("warm_stored")
    idx_copied = sem("idx_copied")
    weights_high = sem("weights_high")
    weights_split = sem("weights_split")
    xgT_full = sem("xgT_full")
    xgT_high = sem("xgT_high")
    xgT_low = sem("xgT_low")
    gu_full = sem("gu_full")
    silu_ready = sem("silu_ready")
    hid_made = sem("hid_made")
    hidT_full = sem("hidT_full")
    hidT_high = sem("hidT_high")
    hidT_low = sem("hidT_low")
    dn_full = sem("dn_full")
    eo_ready = sem("eo_ready")
    added = sem("added")
    rows_added = sem("rows_added")
    passed = sem("passed_e")

    def run(eng, step):
        with eng.Fori(0, ROUNDS - 1) as j:
            for q in range(STEPS):
                step(j, q, 2 * STEPS)
        for q in range(STEPS):
            step(ROUNDS - 1, q, STEPS - 1 - q)

    def later(j, q, d):
        return j + (q + d) // STEPS, (q + d) % STEPS

    def new_rows(q, d, behind):
        return behind >= d and STEP[(q + d) % STEPS][2] != 1

    def rows_of(q):
        return STEP[q][3]

    def hidden_step(j, q):
        return q if isinstance(j, str) else 2 * WARM + j * STEPS + q

    def rows_set(j, i):
        return i if isinstance(j, str) else WARM + j * SETS + i

    def set_of(j, q):
        return q // 2 if isinstance(j, str) else rows_of(q)

    def xgT_slot(j, q):
        return (q // 2) % 2 if isinstance(j, str) else XGT[rows_of(q)]

    def ring_distance(i, ring):
        return ring if i >= ring else next(d for d in range(1, 2 * ring)
                                           if d > i and (i - d + SETS) % ring == i % ring)

    FIRST_WEIGHTS = [("shared", 0), ("shared", 1)] + [("expert", e) for e in range(RING)]

    def weights_at(e):
        return e + 2

    def raw_slot(n):
        return (n + 2) % RAW

    def split_target(kind, n):
        if kind == "shared":
            return tuple(h[:, n, :] for h in sgu), tuple(h[:, n, :] for h in sdn)
        return tuple(h[:, n % RING, :] for h in gu), tuple(h[:, n % RING, :] for h in dn)

    def pieces_of(q, last_round):
        mine = [p for p in range(PIECES * U) if p * STEPS // (PIECES * U) == q]
        for p in mine:
            n = p // PIECES
            assert step_of_expert[n] <= q
            assert q < (step_of_expert[n + RING] if n + RING < U
                        else step_of_expert[n + RING - U] + STEPS) - 2
        named = [(p // PIECES + RING, p % PIECES) for p in mine]
        named = [(n, part) for n, part in named if n < U or not last_round]
        return named[:1], named[1:]

    def warm_pieces(w):
        first = 2 * WARM - PIECES * RING // 2
        if w < first:
            return [], []
        p = 2 * (w - first)
        return [(p // PIECES, p % PIECES)], [((p + 1) // PIECES, (p + 1) % PIECES)]

    def gu_part(part):
        return slice(part * GU // 2, (part + 1) * GU // 2)

    def sync(sp):
        def load(kind, e, slot, order=None):
            guv, dnv = ((t["gate_up"][e], t["down"][e]) if kind == "expert"
                        else (t["shared_gate_up"][e], t["shared_down"][e]))
            for part in range(PIECES):
                loaded = raw_loaded[slot][part]
                if order is not None:
                    sp.wait_ge(weights_split, (order - RAW) * PIECES + part + 1)
                if part < 2:
                    sp.dma_start(gu_raw[:, slot, gu_part(part)].rearrange("p (c n) -> p c n", n=2 * I),
                                 guv[part * D // 2:(part + 1) * D // 2, :]
                                 .rearrange("(c p) n -> p c n", p=P)).then_inc(loaded, 16)
                else:
                    sp.dma_start(dn_raw[:, slot, 0:D], dnv[0:P, :]).then_inc(loaded, 16)
                    sp.dma_start(dn_raw[0:I - P, slot, D:2 * D], dnv[P:I, :]).then_inc(loaded, 16)

        sp.wait_ge(kept.group_full, kept.projected)
        def warm_rows(rows, m):
            return rows[m * P:(m + 1) * P, :]

        sp.dma_start(xg[:, 0, :], warm_rows(x2_rows, 0)).then_inc(warm_loaded[0], 16)
        load(*FIRST_WEIGHTS[0], 0)
        for m in range(1, WARM):
            sp.dma_start(xg[:, m, :], warm_rows(x2_rows, m)).then_inc(warm_loaded[m], 16)
        load(*FIRST_WEIGHTS[1], 1)
        for m in range(2, RAW):
            load(*FIRST_WEIGHTS[m], m)
        sp.wait_ge(kept.rows_ready, 2 * B)
        for m in range(WARM):
            sp.dma_start(eo[:, m, :], warm_rows(t["out"], m)).then_inc(warm_base_loaded, 16)
        for m in range(RAW, len(FIRST_WEIGHTS)):
            load(*FIRST_WEIGHTS[m], m % RAW, m)

        def store_warm(m):
            sp.wait_ge(eo_ready, m + 1)
            sp.dma_start(warm_rows(t["out"], m), eo[:, m, :]).then_inc(warm_stored, 16)

        store_warm(0)
        sp.wait_ge(kept.slots_free, B + 1)
        sp.dma_start(tab[:, :, :].rearrange("p e b -> p (e b)"),
                     table.rearrange("(s e) b -> s (e b)", s=CAP)).then_inc(tab_loaded, 16)
        for m in range(1, WARM):
            store_warm(m)

        def step(j, q, behind):
            kind, n, _, _ = STEP[q]
            if kind == "expert" and (behind >= STEPS or n + RING < U):
                e = j * U + n + RING
                load("expert", e, raw_slot(n + RING), weights_at(e))
        run(sp, step)

    def gpsimd(pool):
        pool.nop().then_inc(rows_added, XG)
        pool.tensor_copy(idx_all[:, E:E + T // P], own[:, :])
        pool.wait_ge(tab_loaded, 16)
        pool.tensor_copy(idx_all[:, 0:E], tab[:, :, 0]).then_inc(idx_ready, 1)

        def column(j, i):
            kind, n = next((kind, n) for kind, n, _, of in STEP if of == i)
            return j * U + n if kind == "expert" else j * G + (E + WARM + n)

        def gather(j, i, copies):
            slot = i % XG
            if not isinstance(j, int) or j or i >= XG:
                wait_alone(pool, xgT_full, rows_set(j, i) + 1 - ring_distance(i, XG), passed)
            pool.tensor_copy(idx_in[:, slot:slot + 1],
                             idx_all[:, bass.ds(column(j, i), 1)]).then_inc(idx_copied, 1)
            wait_alone(pool, idx_copied, copies, passed)
            pool.indirect_dma_start(
                out=xg[:, slot, :], out_offset=None, in_=x2_rows,
                in_offset=bass.IndirectOffsetOnAxis(ap=idx_in[:, slot:slot + 1], axis=0)
            ).then_inc(gathered[slot], 16)

        def copy_idx_out(j, i, copies):
            slot = i % XG
            pool.tensor_copy(idx_out[:, slot:slot + 1],
                             idx_all[:, bass.ds(column(j, i), 1)]).then_inc(idx_copied, 1)
            wait_alone(pool, idx_copied, copies, passed)

        pool.wait_ge(idx_ready, 1)
        pool.wait_ge(xgT_full, WARM)
        for i in range(AHEAD):
            gather(0, i, i + 1)
        copy_idx_out(0, 0, AHEAD + 1)
        pool.wait_ge(warm_stored, 16 * WARM)

        def step(j, q, behind):
            i = rows_of(q)
            if STEP[q][2] == 0:
                return
            r = j * SETS + i
            in_loop = behind >= STEPS
            copies = AHEAD + 1 + (2 * r if in_loop else
                                  2 * (ROUNDS - 1) * SETS + i + min(i, SETS - AHEAD))
            wait_alone(pool, eo_ready, WARM + r + 1, passed)
            slot = i % XG
            pool.indirect_dma_start(
                out=t["out"], out_offset=bass.IndirectOffsetOnAxis(ap=idx_out[:, slot:slot + 1], axis=0),
                in_=eo[:, slot, :], in_offset=None, compute_op=ALU.add).then_inc(added, 16)
            if in_loop or i + AHEAD < SETS:
                gather(j + (i + AHEAD) // SETS, (i + AHEAD) % SETS, copies + 1)
                copies = copies + 1
            if in_loop or i + 1 < SETS:
                copy_idx_out(j + (i + 1) // SETS, (i + 1) % SETS, copies + 1)
            pool.wait_ge(added, (r + 1) * 16)
            pool.sem_inc(rows_added, 1)
        run(pool, step)

    def scalar(act):
        def piece(kind, n, part, slot, loads):
            to_gu, to_dn = split_target(kind, n)
            act.wait_ge(raw_loaded[slot][part], loads * (16 if part < 2 else 32))
            if part < 2:
                act.activation(to_gu[0][:, gu_part(part)], gu_raw[:, slot, gu_part(part)],
                               ACT.Copy).then_inc(weights_high, 1)
            else:
                act.activation(to_dn[0][:, 0:D], dn_raw[:, slot, 0:D], ACT.Copy)
                act.activation(to_dn[0][0:I - P, D:2 * D], dn_raw[0:I - P, slot, D:2 * D],
                               ACT.Copy).then_inc(weights_high, 1)

        def split_pieces(pieces, rounds=0):
            for n, part in pieces:
                piece("expert", n, part, raw_slot(n), rounds * (U // RAW) + (n + 2) // RAW + 1)

        def high_xgT(j, q):
            i = set_of(j, q)
            act.wait_ge(xgT_full, rows_set(j, i) + 1)
            act.activation(xgT[0][:, xgT_slot(j, q), :], ps_xgT[:, i % 2, :], ACT.Copy).then_inc(xgT_high, 1)

        def high_hidT(j, q):
            act.wait_ge(hidT_full, hidden_step(j, q) + 1)
            act.activation(hidT[0][:, q % 2, :], ps_hidT[:, q % 2, 0:HP], ACT.Copy).then_inc(hidT_high, 1)

        def gate(j, q):
            act.wait_ge(gu_full, hidden_step(j, q) + 1)
            act.activation(silu[:, q % 2, :], ps_gu[:, q % 2, 0:I], ACT.Silu).then_inc(silu_ready, 1)

        for half in range(2):
            for part in range(PIECES):
                piece("shared", half, part, half, 1)
        high_xgT("warm", 0)
        high_xgT("warm", 2)
        gate("warm", 0)
        gate("warm", 1)
        high_hidT("warm", 0)
        for w in range(2 * WARM):
            if w + 1 < 2 * WARM:
                high_hidT("warm", w + 1)
            if w + 1 == 2 * WARM:
                high_xgT(0, 0)
                high_xgT(0, 1)
            before_gate, behind_gate = warm_pieces(w)
            split_pieces(before_gate)
            if w + 2 < 2 * WARM:
                gate("warm", w + 2)
            split_pieces(behind_gate)
            if w % 2 == 0 and w + 4 < 2 * WARM:
                high_xgT("warm", w + 4)

        gate(0, 0)
        high_xgT(0, 2)
        gate(0, 1)
        high_xgT(0, 3)
        high_hidT(0, 0)
        act.wait_ge(warm_stored, 16 * WARM)

        def step(j, q, behind):
            kind, n, half, i = STEP[q]
            if behind >= 1:
                high_hidT(*later(j, q, 1))
            if half != 0:
                r = j * SETS + i
                act.wait_ge(dn_full, WARM + r + 1)
                act.wait_ge(rows_added, r + (1 + XG - ring_distance(i, XG)))
                scale = tab[:, bass.ds(j * U + n, 1), 1] if kind == "expert" else 1.0
                act.activation(eo[:, i % XG, :], ps_dn[:, i % 2, :], ACT.Copy,
                               scale=scale).then_inc(eo_ready, 1)
            before_gate, behind_gate = pieces_of(q, behind < STEPS)
            split_pieces(before_gate, j)
            if behind >= 2:
                gate(*later(j, q, 2))
            split_pieces(behind_gate, j)
            if new_rows(q, 4, behind):
                high_xgT(*later(j, q, 4))
        run(act, step)

    def vector(dve):
        def subtract(lo, x, hi):
            return dve.tensor_tensor(lo, x, hi.bitcast(F32), ALU.subtract)

        def piece(kind, n, part, slot, order):
            to_gu, to_dn = split_target(kind, n)
            dve.wait_ge(weights_high, order * PIECES + part + 1)
            if part < 2:
                last = subtract(to_gu[1][:, gu_part(part)], gu_raw[:, slot, gu_part(part)],
                                to_gu[0][:, gu_part(part)])
            else:
                subtract(to_dn[1], dn_raw[:, slot, 0:D], to_dn[0][:, 0:D])
                last = subtract(to_dn[0][I - P:P, D:2 * D], dn_raw[0:I - P, slot, D:2 * D],
                                to_dn[0][0:I - P, D:2 * D])
            last.then_inc(weights_split, 1)

        def split_pieces(pieces, rounds=0):
            for n, part in pieces:
                piece("expert", n, part, raw_slot(n), weights_at(rounds * U + n))

        def low_xgT(j, q):
            i = set_of(j, q)
            slot = xgT_slot(j, q)
            dve.wait_ge(xgT_high, rows_set(j, i) + 1)
            subtract(xgT[1][:, slot, :], ps_xgT[:, i % 2, :], xgT[0][:, slot, :]).then_inc(xgT_low, 1)

        def low_hidT(j, q):
            dve.wait_ge(hidT_high, hidden_step(j, q) + 1)
            subtract(hidT[1][:, q % 2, :], ps_hidT[:, q % 2, 0:HP], hidT[0][:, q % 2, :]).then_inc(hidT_low, 1)

        def up(j, q):
            dve.wait_ge(silu_ready, hidden_step(j, q) + 1)
            dve.tensor_tensor(hid[:, q % 2, 0:I], silu[:, q % 2, :], ps_gu[:, q % 2, I:2 * I], ALU.mult)
            dve.tensor_tensor(hid[:, q % 2, I:HP], silu[:, q % 2, P:I], ps_gu[:, q % 2, I + P:2 * I],
                              ALU.mult).then_inc(hid_made, 1)

        low_xgT("warm", 0)
        for half in range(2):
            for part in range(PIECES):
                piece("shared", half, part, half, half)
        low_xgT("warm", 2)
        up("warm", 0)
        up("warm", 1)
        low_hidT("warm", 0)
        dve.wait_ge(warm_base_loaded, 16 * WARM)
        for w in range(2 * WARM):
            if w + 1 < 2 * WARM:
                low_hidT("warm", w + 1)
            if w + 1 == 2 * WARM:
                low_xgT(0, 0)
                low_xgT(0, 1)
            split_pieces(warm_pieces(w - 1)[1])
            if w + 2 < 2 * WARM:
                up("warm", w + 2)
            split_pieces(warm_pieces(w)[0])
            if w % 2 == 0 and w + 4 < 2 * WARM:
                low_xgT("warm", w + 4)
            if w % 2 == 1:
                m = w // 2
                dve.wait_ge(dn_full, m + 1)
                dve.tensor_tensor(eo[:, m, :], ps_dn[:, m % 2, :], eo[:, m, :], ALU.add).then_inc(eo_ready, 1)

        up(0, 0)
        low_xgT(0, 2)
        up(0, 1)
        low_xgT(0, 3)
        low_hidT(0, 0)

        def step(j, q, behind):
            if behind >= 1:
                low_hidT(*later(j, q, 1))
            if q == 0:
                split_pieces([(n - U, part) for n, part in pieces_of(STEPS - 1, False)[1]], j)
            else:
                split_pieces(pieces_of(q - 1, behind < STEPS)[1], j)
            if behind >= 2:
                up(*later(j, q, 2))
            split_pieces(pieces_of(q, behind < STEPS)[0], j)
            if new_rows(q, 4, behind):
                low_xgT(*later(j, q, 4))
        run(dve, step)

    def tensor(pe):
        def cols(n, width=P):
            return slice(n * width, (n + 1) * width)

        def weights(j, q):
            if isinstance(j, str):
                return split_target("shared", q % 2)
            kind, n, half, _ = STEP[q]
            return split_target(kind, n if kind == "expert" else half)

        def wait_for_pieces(j, q, pieces):
            if isinstance(j, str):
                pe.wait_ge(weights_split, q % 2 * PIECES + pieces)
            elif STEP[q][0] == "expert":
                pe.wait_ge(weights_split, weights_at(j * U + STEP[q][1]) * PIECES + pieces)

        def transpose_rows(j, q):
            i = set_of(j, q)
            if isinstance(j, str):
                pe.wait_ge(warm_loaded[i], 16)
            else:
                uses = len(range(i % XG, SETS, XG))
                pe.wait_ge(gathered[i % XG], j * (uses * 16) + (i // XG + 1) * 16)
            for c in range(C):
                last = pe.transpose(ps_xgT[:, i % 2, cols(c)], xg[:, i % XG, cols(c)], ident[:, :])
            last.then_inc(xgT_full, 1)

        def gate_up(j, q):
            pe.wait_ge(xgT_low, rows_set(j, set_of(j, q)) + 1)
            wait_for_pieces(j, q, 2)
            w_gu, _ = weights(j, q)
            for c in range(C):
                last = product(pe, ps_gu[:, q % 2, 0:2 * I], [h[:, xgT_slot(j, q), cols(c)] for h in xgT],
                               [h[:, cols(c, 2 * I)] for h in w_gu], c == 0, c == C - 1)
            last.then_inc(gu_full, 1)

        def transpose_hidden(j, q):
            pe.wait_ge(hid_made, hidden_step(j, q) + 1)
            for c in range(2):
                last = pe.transpose(ps_hidT[:, q % 2, cols(c)], hid[:, q % 2, cols(c)], ident[:, :])
            last.then_inc(hidT_full, 1)

        def down(j, q):
            i = set_of(j, q)
            half = q % 2 if isinstance(j, str) else STEP[q][2]
            pe.wait_ge(hidT_low, hidden_step(j, q) + 1)
            wait_for_pieces(j, q, PIECES)
            if not isinstance(j, str):
                pe.wait_ge(eo_ready, rows_set(j, i) + 1 - ring_distance(i, 2))
            elif i >= 2:
                pe.wait_ge(eo_ready, i - 1)
            out = ps_dn[:, i % 2, :]
            (h_hi, h_lo), (w_hi, w_lo) = [h[:, q % 2, :] for h in hidT], weights(j, q)[1]
            product(pe, out, (h_hi[:, 0:P], h_lo[:, 0:P]), (w_hi[:, 0:D], w_lo), half != 1, False)
            pe.matmul(out, h_hi[:, P:HP], w_hi[:, D:2 * D], start=False, stop=False)
            last = pe.matmul(out, h_lo[0:I - P, P:HP], w_hi[0:I - P, D:2 * D], start=False, stop=half != 0)
            if half != 0:
                last.then_inc(dn_full, 1)

        transpose_rows("warm", 0)
        transpose_rows("warm", 2)
        gate_up("warm", 0)
        gate_up("warm", 1)
        transpose_hidden("warm", 0)
        for w in range(2 * WARM):
            down("warm", w)
            if w + 1 < 2 * WARM:
                transpose_hidden("warm", w + 1)
            if w + 2 < 2 * WARM:
                gate_up("warm", w + 2)
            if w % 2 == 0 and w + 4 < 2 * WARM:
                transpose_rows("warm", w + 4)
            if w + 2 == 2 * WARM:
                transpose_rows(0, 0)
                transpose_rows(0, 1)

        gate_up(0, 0)
        transpose_rows(0, 2)
        gate_up(0, 1)
        transpose_rows(0, 3)
        transpose_hidden(0, 0)

        def step(j, q, behind):
            down(j, q)
            if behind >= 1:
                transpose_hidden(*later(j, q, 1))
            if behind >= 2:
                gate_up(*later(j, q, 2))
            if new_rows(q, 4, behind):
                transpose_rows(*later(j, q, 4))
        run(pe, step)

    return Programs(sync, gpsimd, scalar, vector, tensor)


class Programs:

    def __init__(self, sync, gpsimd, scalar, vector, tensor):
        self.sync, self.gpsimd, self.scalar, self.vector, self.tensor = sync, gpsimd, scalar, vector, tensor


class Kept:
    pass


def build(nc, t):
    table = nc.dram_tensor("table", (E * CAP, 2), F32, kind="Internal").ap()
    x2_rows = nc.dram_tensor("x2_rows", (ROWS, D), F32, kind="Internal").ap()
    with ExitStack() as ctx:
        def sem(name):
            return ctx.enter_context(nc.semaphore(name))

        kept = Kept()
        kept.ident = ctx.enter_context(nc.sbuf_tensor("ident", [P, P], F32))
        kept.own = ctx.enter_context(nc.sbuf_tensor("own", [P, T // P], F32))
        kept.slot = ctx.enter_context(nc.sbuf_tensor("slot", [P, NT, K], I32))
        kept.rows = ctx.enter_context(nc.sbuf_tensor("rows", [P, NT, K, 2], F32))
        with ExitStack() as memory:
            one = attention_and_router(nc, memory, sem, t, table, x2_rows, kept)
        with ExitStack() as memory:
            two = experts(nc, memory, sem, t, table, x2_rows, kept)
            block = memory.enter_context(nc.Block())

            @block.sync
            def _(sp):
                one.sync(sp)
                two.sync(sp)

            @block.gpsimd
            def _(pool):
                one.gpsimd(pool)
                two.gpsimd(pool)

            @block.scalar
            def _(act):
                one.scalar(act)
                two.scalar(act)

            @block.vector
            def _(dve):
                one.vector(dve)
                two.vector(dve)

            @block.tensor
            def _(pe):
                one.tensor(pe)
                two.tensor(pe)


def kernel(x, ctx_2048, mask_BxSx4224_bf0, L0_xattn_wq, L0_xattn_wk, L0_xattn_wv, L0_xattn_wo,
           L0_ffn_gate_w, L0_ffn_gate_up_proj, L0_ffn_down_proj, L0_ffn_shared_gate_w,
           L0_ffn_shared_up_w, L0_ffn_shared_down_w):
    import concourse.bacc as bacc
    from concourse.bass_utils import run_bass_kernel_spmd

    def chunked(w):
        n = w.shape[1]
        return np.ascontiguousarray(w.reshape(-1, P, n).transpose(1, 0, 2).reshape(P, -1))

    def arr(a):
        return np.asarray(a)

    context = arr(ctx_2048)
    arrays = {
        "x": np.ascontiguousarray(arr(x).reshape(T, D)),
        "ctx": np.ascontiguousarray(context.reshape(T, D)),
        "ctxT": np.stack([chunked(context[b].T) for b in range(B)]),
        "wqT": chunked(arr(L0_xattn_wq).T),
        "wkT": chunked(arr(L0_xattn_wk).T),
        "wvT": chunked(arr(L0_xattn_wv).T),
        "woT": chunked(arr(L0_xattn_wo).T),
        "gateT": chunked(arr(L0_ffn_gate_w).T),
        "shared_gate_up": np.stack([np.concatenate(
            [arr(L0_ffn_shared_gate_w)[h * I:(h + 1) * I].T, arr(L0_ffn_shared_up_w)[h * I:(h + 1) * I].T],
            axis=1) for h in range(2)]),
        "shared_down": np.ascontiguousarray(arr(L0_ffn_shared_down_w).T).reshape(2, I, D),
        "gate_up": np.ascontiguousarray(arr(L0_ffn_gate_up_proj)),
        "down": np.ascontiguousarray(arr(L0_ffn_down_proj)),
    }
    nc = bacc.Bacc("TRN2", target_bir_lowering=False, num_devices=1)
    t = {name: nc.dram_tensor(name + "_in", a.shape, mybir.dt.from_np(a.dtype), kind="ExternalInput").ap()
         for name, a in arrays.items()}
    t["out"] = nc.dram_tensor("out_rows", (ROWS, D), F32, kind="ExternalOutput").ap()
    build(nc, t)
    r = run_bass_kernel_spmd(nc, [{name + "_in": a for name, a in arrays.items()}], core_ids=[0])
    return r.results[0]["out_rows"][0:T].reshape(B, S, D)
```
